# Optimizing a Trainium2 kernel written in Bass

```python
import numpy as np
import jax
import jax.numpy as jnp

def _softmax(x, axis=-1):
    return jax.nn.softmax(x, axis=axis)

def _gelu(x):
    return jax.nn.gelu(x, approximate=True)

def _silu(x):
    return jax.nn.silu(x)

def _sigmoid(x):
    return jax.nn.sigmoid(x)

def _layernorm(x, axis=-1, eps=1e-05):
    m = jnp.mean(x, axis=axis, keepdims=True)
    v = jnp.var(x, axis=axis, keepdims=True)
    return (x - m) / jnp.sqrt(v + eps)

def _scatter_add(tgt, idx, src, axis=0):
    return tgt.at[idx].add(src)

def _segment_sum(src, seg, n):
    return jax.ops.segment_sum(src, seg, n)
kernel_name = 'mk_perceiver_d1_seqx_r2_da6091'

def setup_inputs(seed: int=0):
    np.random.seed(seed)
    _w = jnp.asarray

    def _rec_inputs():
        import jax
        import jax.numpy as jnp
        _rk = jax.random.key(seed)
        x = -0.0003929 + 0.9999 * jax.random.normal(jax.random.fold_in(_rk, 1), (4, 128, 512), jnp.float32)
        _lenS = 128 - jax.random.randint(jax.random.fold_in(_rk, 7), (4,), 0, max(1, 128 // 4) + 1, jnp.int32)
        _lenS2 = 2048 - jax.random.randint(jax.random.fold_in(_rk, 8), (4,), 0, max(1, 2048 // 4) + 1, jnp.int32)
        _ctx_512P = jax.random.normal(jax.random.fold_in(_rk, 11), (4, 16, 256), jnp.float32)
        _ctx_512c = jax.random.dirichlet(jax.random.fold_in(_rk, 511), 0.3 * jnp.ones((16,), jnp.float32), (4, 2048))
        _ctx_512t = jnp.einsum('bsk,bkd->bsd', _ctx_512c, _ctx_512P)
        _ctx_512t = _ctx_512t * jax.lax.rsqrt(jnp.mean(jnp.square(_ctx_512t)) + 1e-12) * 0.953939
        ctx_512 = 4.13588e-05 + 0.999923 * (_ctx_512t + 0.3 * jax.random.normal(jax.random.fold_in(_rk, 611), (4, 2048, 256), jnp.float32))
        return (x, ctx_512)
    x, ctx_512 = _rec_inputs()

    def _L0_xattn_setup():
        import jax, jax.numpy as jnp
        import numpy as np
        B, LQ, LK = (8, 1024, 1024)
        QD, KD, VD = (512, 256, 256)
        key = jax.random.key(seed)
        ks = jax.random.split(key, 9)
        s = 0.02
        return {'query': jax.random.normal(ks[0], (B, LQ, QD), jnp.float32), 'key': jax.random.normal(ks[1], (B, LK, KD), jnp.float32), 'value': jax.random.normal(ks[2], (B, LK, VD), jnp.float32), 'Wq': jax.random.normal(ks[3], (QD, QD), jnp.float32) * s, 'bq': jnp.zeros((QD,), jnp.float32), 'Wk': jax.random.normal(ks[4], (KD, QD), jnp.float32) * s, 'bk': jnp.zeros((QD,), jnp.float32), 'Wv': jax.random.normal(ks[5], (VD, QD), jnp.float32) * s, 'bv': jnp.zeros((QD,), jnp.float32)}
    _L0_xattn_all = _L0_xattn_setup()
    _L0_xattn_in = {k: v for k, v in _L0_xattn_all.items() if k in ('Wq', 'bq', 'Wk', 'bk', 'Wv', 'bv')}
    del _L0_xattn_all

    def _L0_attn_setup():
        import jax, jax.numpy as jnp
        import numpy as np
        B, L, H, N = (4, 2048, 512, 64)
        LK = 256

        def _dss_kernel(Lambda_re, Lambda_im, log_dt, W_re, W_im, Lk):
            dt = jnp.exp(log_dt)
            Lam = -jnp.exp(Lambda_re) + 1j * Lambda_im
            dtLam = dt[:, None] * Lam[None, :]
            P = dtLam[:, :, None] * jnp.arange(Lk, dtype=jnp.float32)
            S = jnp.exp(P)
            W = W_re + 1j * W_im
            k = jnp.einsum('hn,hnl->lh', W, S).real
            return k
        key = jax.random.key(seed)
        ks = jax.random.split(key, 7)
        u = jax.random.normal(ks[0], (B, L, H), jnp.float32)
        D = jax.random.normal(ks[1], (H,), jnp.float32)
        Lambda_re = jax.random.normal(ks[2], (N,), jnp.float32) * 0.5
        Lambda_im = jax.random.normal(ks[3], (N,), jnp.float32) * np.pi
        log_dt = jax.random.uniform(ks[4], (H,), jnp.float32, minval=np.log(0.001), maxval=np.log(0.1))
        W_re = jax.random.normal(ks[5], (H, N), jnp.float32) / np.sqrt(N)
        W_im = jax.random.normal(ks[6], (H, N), jnp.float32) / np.sqrt(N)
        return dict(u=u, D=D, Lambda_re=Lambda_re, Lambda_im=Lambda_im, log_dt=log_dt, W_re=W_re, W_im=W_im)
    _L0_attn_all = _L0_attn_setup()
    _L0_attn_in = {k: v for k, v in _L0_attn_all.items() if k in ('D', 'Lambda_re', 'Lambda_im', 'log_dt', 'W_re', 'W_im')}
    del _L0_attn_all

    def _L0_ffn_setup():
        import jax, jax.numpy as jnp
        import numpy as np
        D_MODEL = 512
        MLP_DIM = 2048
        N_EXPERTS = 8
        B, T = (4, 512)
        key = jax.random.key(seed)
        ks = jax.random.split(key, 7)
        scale_in = (1.0 / D_MODEL) ** 0.5
        scale_out = (1.0 / MLP_DIM) ** 0.5
        bound_g = (1.0 / D_MODEL) ** 0.5
        w_gate = jax.random.uniform(ks[0], (D_MODEL, N_EXPERTS), minval=-bound_g, maxval=bound_g, dtype=jnp.float32)
        b_gate = jax.random.uniform(ks[1], (N_EXPERTS,), minval=-bound_g, maxval=bound_g, dtype=jnp.float32)
        W1 = jax.random.uniform(ks[2], (N_EXPERTS, D_MODEL, MLP_DIM), minval=-scale_in, maxval=scale_in, dtype=jnp.float32)
        b1 = jnp.zeros((N_EXPERTS, MLP_DIM), dtype=jnp.float32)
        W2 = jax.random.uniform(ks[3], (N_EXPERTS, MLP_DIM, D_MODEL), minval=-scale_out, maxval=scale_out, dtype=jnp.float32)
        b2 = jnp.zeros((N_EXPERTS, D_MODEL), dtype=jnp.float32)
        x = jax.random.normal(ks[4], (B, T, D_MODEL), dtype=jnp.float32)
        return {'x': x, 'w_gate': w_gate, 'b_gate': b_gate, 'W1': W1, 'b1': b1, 'W2': W2, 'b2': b2}
    _L0_ffn_all = _L0_ffn_setup()
    _L0_ffn_in = {k: v for k, v in _L0_ffn_all.items() if k in ('w_gate', 'b_gate', 'W1', 'b1', 'W2', 'b2')}
    del _L0_ffn_all
    return {'x': x, 'ctx_512': ctx_512, 'L0_xattn_Wq': _L0_xattn_in['Wq'], 'L0_xattn_bq': _L0_xattn_in['bq'], 'L0_xattn_Wk': _L0_xattn_in['Wk'], 'L0_xattn_bk': _L0_xattn_in['bk'], 'L0_xattn_Wv': _L0_xattn_in['Wv'], 'L0_xattn_bv': _L0_xattn_in['bv'], 'L0_attn_D': _L0_attn_in['D'], 'L0_attn_Lambda_re': _L0_attn_in['Lambda_re'], 'L0_attn_Lambda_im': _L0_attn_in['Lambda_im'], 'L0_attn_log_dt': _L0_attn_in['log_dt'], 'L0_attn_W_re': _L0_attn_in['W_re'], 'L0_attn_W_im': _L0_attn_in['W_im'], 'L0_ffn_w_gate': _L0_ffn_in['w_gate'], 'L0_ffn_b_gate': _L0_ffn_in['b_gate'], 'L0_ffn_W1': _L0_ffn_in['W1'], 'L0_ffn_b1': _L0_ffn_in['b1'], 'L0_ffn_W2': _L0_ffn_in['W2'], 'L0_ffn_b2': _L0_ffn_in['b2']}

def reference(x, ctx_512, L0_xattn_Wq, L0_xattn_bq, L0_xattn_Wk, L0_xattn_bk, L0_xattn_Wv, L0_xattn_bv, L0_attn_D, L0_attn_Lambda_re, L0_attn_Lambda_im, L0_attn_log_dt, L0_attn_W_re, L0_attn_W_im, L0_ffn_w_gate, L0_ffn_b_gate, L0_ffn_W1, L0_ffn_b1, L0_ffn_W2, L0_ffn_b2):
    import jax
    import jax.numpy as jnp

    def _L0_xattn_ref(query, key, value, Wq, bq, Wk, bk, Wv, bv):
        import jax, jax.numpy as jnp
        import numpy as np
        B, LQ, LK = (8, 1024, 1024)
        QD, KD, VD = (512, 256, 256)
        q = jnp.einsum('bld,de->ble', query, Wq) + bq
        k = jnp.einsum('bld,de->ble', key, Wk) + bk
        v = jnp.einsum('bld,de->ble', value, Wv) + bv
        scores = jnp.einsum('bqe,bke->bqk', q, k)
        attn = jax.nn.softmax(scores, axis=-1)
        out = jnp.einsum('bqk,bke->bqe', attn, v)
        return out

    def _L0_attn_ref(u, D, Lambda_re, Lambda_im, log_dt, W_re, W_im):
        import jax, jax.numpy as jnp
        import numpy as np
        B, L, H, N = (4, 2048, 512, 64)
        LK = 256

        def _dss_kernel(Lambda_re, Lambda_im, log_dt, W_re, W_im, Lk):
            dt = jnp.exp(log_dt)
            Lam = -jnp.exp(Lambda_re) + 1j * Lambda_im
            dtLam = dt[:, None] * Lam[None, :]
            P = dtLam[:, :, None] * jnp.arange(Lk, dtype=jnp.float32)
            S = jnp.exp(P)
            W = W_re + 1j * W_im
            k = jnp.einsum('hn,hnl->lh', W, S).real
            return k
        Lseq = u.shape[1]
        Lk = min(LK, Lseq)
        k = _dss_kernel(Lambda_re, Lambda_im, log_dt, W_re, W_im, Lk)
        n = Lseq + Lk
        k_f = jnp.fft.rfft(k, n=n, axis=0)
        u_f = jnp.fft.rfft(u, n=n, axis=1)
        y = jnp.fft.irfft(k_f[None, :, :] * u_f, n=n, axis=1)[:, :Lseq, :]
        return y + u * D[None, None, :]

    def _L0_ffn_ref(x, w_gate, b_gate, W1, b1, W2, b2):
        import jax, jax.numpy as jnp
        import numpy as np
        D_MODEL = 512
        MLP_DIM = 2048
        N_EXPERTS = 8
        B, T = (4, 512)
        b, t, d = x.shape
        x_flat = x.reshape(b * t, d)
        logits = x_flat @ w_gate + b_gate
        probs = jax.nn.softmax(logits, axis=-1)
        route_p = jnp.max(probs, axis=-1)
        route_idx = jnp.argmax(probs, axis=-1)
        h = jnp.einsum('nd,edm->enm', x_flat, W1) + b1[:, None, :]
        h = jax.nn.relu(h)
        y = jnp.einsum('enm,emd->end', h, W2) + b2[:, None, :]
        n = b * t
        out = y[route_idx, jnp.arange(n)] * route_p[:, None]
        return out.reshape(b, t, d)
    x = x + _L0_xattn_ref(_layernorm(x, axis=-1), ctx_512, ctx_512, L0_xattn_Wq, L0_xattn_bq, L0_xattn_Wk, L0_xattn_bk, L0_xattn_Wv, L0_xattn_bv)
    x = x + _L0_attn_ref(_layernorm(x, axis=-1), L0_attn_D, L0_attn_Lambda_re, L0_attn_Lambda_im, L0_attn_log_dt, L0_attn_W_re, L0_attn_W_im)
    x = x + _L0_ffn_ref(_layernorm(x, axis=-1), L0_ffn_w_gate, L0_ffn_b_gate, L0_ffn_W1, L0_ffn_b1, L0_ffn_W2, L0_ffn_b2)
    return x

_drawn_inputs = setup_inputs


def setup_inputs(seed=0):
    import zlib

    import numpy as np

    out = dict(_drawn_inputs(seed))
    spreads = {'L0_xattn_bq': (0.0, 0.1),
     'L0_xattn_bk': (0.0, 0.8),
     'L0_xattn_bv': (0.0, 0.1),
     'L0_ffn_b1': (0.0, 0.8),
     'L0_ffn_b2': (0.0, 0.8)}
    factors = {'L0_ffn_w_gate': 8.0, 'L0_ffn_b_gate': 8.0, 'L0_ffn_W1': 8.0, 'L0_ffn_W2': 8.0}
    for name, (base, spread) in spreads.items():
        noise = np.random.default_rng([zlib.crc32(name.encode()), seed]).standard_normal(out[name].shape)
        drawn = base * np.exp(spread * noise) if base else spread * noise
        out[name] = jnp.asarray(drawn.astype(out[name].dtype))
    for name, factor in factors.items():
        out[name] = (out[name] * factor).astype(out[name].dtype)
    return out
```

```python
from contextlib import ExitStack

import concourse.bass as bass
from concourse import mybir

F32 = mybir.dt.float32
I32 = mybir.dt.int32
U32 = mybir.dt.uint32
ALU = mybir.AluOpType
ACT = mybir.ActivationFunctionType
AX = mybir.AxisListType.X

P = 128
NB, LQ, D = 4, 128, 512
LK, DC = 2048, 256
NS = 64
NE, DM = 8, 2048
DCH, CCH, MCH = D // P, DC // P, DM // P
KCH = LK // P
NQ = 4
KPQ = KCH // NQ
AH, BL = 16, 8
HG = P // AH
SLOT = 64
MINW = NB * LQ // SLOT
MAXW = NE + (NB * LQ - NE) // SLOT
NSLOT = 10
UNITS = 4
EPS = 1e-5
ROUND = 1.5 * 2.0 ** 23
TWO_PI = 6.283185307179586

TABLES = {}
_at = 0
for _name, _n in (("ident", P), ("ones", P), ("cos_f", P), ("sin_f", P), ("cos_t", P), ("sin_t", P),
                  ("pick", P + BL - 1), ("own", HG), ("earlier", P), ("iota", SLOT), ("rank_e", NE),
                  ("before_e", (NE + 1) * NE), ("steps", AH + BL), ("phase", 3)):
    TABLES[_name] = (_at, _at + _n)
    _at += _n
TABLE_COLS = _at
COLS = 150

S_BANK = [0, 1, 2, 3]
T0, T1, T2, O_BANK = 4, 5, 6, 7
HA, HB, YB, YT, XW = 0, 1, 2, 3, 7

FILLS = [(S_BANK[d], ("wqk", d)) for d in range(DCH)] + [(O_BANK, ("bias",))]
FILLS += [((T0, T1, T2, T0)[b], ("xnT", b)) for b in range(NB)]
FILLS += [(S_BANK[c], ("q", c)) for c in range(CCH)] + [(O_BANK, ("qb",))]


def _context_fills(b, j):
    return [(T0, ("ct", b, j, 0)), (T1, ("ct", b, j, 1)), (S_BANK[j], ("s", b, j))]


def _kernel_fills():
    out = [((T0, T1)[g % 2], ("k1", g)) for g in range(8)]
    return out + [(T2, ("k2",)), (T0, ("k3", 0)), (T1, ("k3", 1))]


def _value_fills(b):
    return [(T2, ("anT", b)), (T0, ("av", b))]


def _freq_fills(b):
    return [(T1, ("uc", b)), (T2, ("us", b))]


def _time_fills(b):
    return [(T0, ("y", b))]


def _gate_fills(b):
    return [(T1, ("x2T", b)), (T2, ("lg", b))]


for _j in range(NQ):
    FILLS += _context_fills(0, _j)
for _b in range(NB):
    for _j in range(NQ):
        FILLS.append((T2, ("pT", _b, _j)))
        if _b + 1 < NB:
            FILLS += _context_fills(_b + 1, _j)
    if _b == 1:
        FILLS += _kernel_fills()
    if _b >= 1:
        FILLS += _value_fills(_b - 1)
    if _b >= 2:
        FILLS += _time_fills(_b - 2)
    FILLS.append((O_BANK, ("pv", _b)))
    if _b >= 1:
        FILLS += _freq_fills(_b - 1)
    if _b >= 2:
        FILLS += _gate_fills(_b - 2)
FILLS += (_value_fills(3) + _time_fills(2) + _freq_fills(3) + _gate_fills(2) + _time_fills(3)
          + _gate_fills(3) + [(T0, ("route",))])

FILL_NO = {}
_count = [0] * 8
for _bank, _what in FILLS:
    _count[_bank] += 1
    FILL_NO[_what] = (_bank, _count[_bank])


def perceiver_layer(nc, x, ctx, wq_t, wk_t, bkq, wv, bv, log_dt, w_ri, lam, d_skip,
                    w_gate, b_gate, w1, b1, w2, b2, tables, out):
    x_rows = x.rearrange("(b t) h -> t b h", t=P)
    out_rows = out.rearrange("(b t) h -> t b h", t=P)
    y_rows = nc.dram_tensor("y_rows", ((MAXW + 1) * SLOT, D), F32, kind="Internal").ap()

    with ExitStack() as stack:
        def sb(name, shape, dt=F32):
            return stack.enter_context(nc.sbuf_tensor(name, shape, dt))

        def sem(name):
            return stack.enter_context(nc.semaphore(name))

        bank = stack.enter_context(nc.psum_tensor("bank", [P, 8, 512], F32))

        ring = sb("ring", [P, NSLOT, 4096])
        x_sb = sb("x_sb", [P, NB, D])
        work = sb("work", [P, 4096])
        kfreq = sb("kfreq", [P, 2, D])
        wri = sb("wri", [P, 2, D])
        dt_sb = sb("dt_sb", [P, D])
        hbuf = sb("hbuf", [P, 1024])
        small = sb("small", [P, 1024])
        tab = sb("tab", [P, TABLE_COLS])
        cols = sb("cols", [P, COLS])
        icols = sb("icols", [P, 16], I32)

        def table(name):
            lo, hi = TABLES[name]
            return tab[:, lo:hi]

        ident, ones = table("ident"), table("ones")

        ctx_sb = [ring[:, b, :].rearrange("p (k c) -> p k c", k=KCH) for b in range(NB)]
        a_sin = ring[:, 2:4, :].rearrange("p s (a h) -> p (s a) h", h=D)
        a_tab = ring[:, 6:8, :].rearrange("p s (a h) -> p (s a) h", h=D)
        b_tab = ring[:, 4, :].rearrange("p (b h) -> p b h", h=D)
        b_sin1 = ring[:, 5, :].rearrange("p (b h) -> p b h", h=D)
        k_parts = ring[:, 5, :].rearrange("p (b h) -> p b h", h=D)
        b_sin2 = work[:].rearrange("p (b h) -> p b h", h=D)
        xn2 = work[:, 0:2048].rearrange("p (b h) -> p b h", h=D)
        y_cos, y_sin, prod1, prod2 = (work[:, 2048 + i * D:2560 + i * D] for i in range(4))
        scratch = ring[:, 8:10, :].rearrange("p s n -> p (s n)")
        xn1 = scratch[:, 0:2048].rearrange("p (b h) -> p b h", h=D)
        probs = scratch[:, 0:2048]
        xn1_t = scratch[:, 2048:4096].rearrange("p (c n) -> p c n", c=DCH)
        probs_t = scratch[:, 2048:4096].rearrange("p (k n) -> p k n", k=KCH)
        wq_sb = scratch[:, 4096:6144].rearrange("p (e d) -> p e d", e=DCH)
        ctx_t = scratch[:, 4096:6144].rearrange("p (u c n) -> p u c n", u=2, c=CCH)
        wk_sb = scratch[:, 6144:7168].rearrange("p (e c) -> p e c", e=DCH)
        q_t = scratch[:, 6144:7168].rearrange("p (c n) -> p c n", c=CCH)
        wqk = scratch[:, 7168:8192].rearrange("p (d c) -> p d c", d=DCH)
        bv_sb = kfreq[:, 0, :]
        u_sb = wri[:, 0, :]
        xn2_t = wri[:, 1, :].rearrange("p (c n) -> p c n", c=DCH)
        an = dt_sb[:, 0:DC]
        an_t = dt_sb[:, DC:2 * DC].rearrange("p (c n) -> p c n", c=CCH)
        onehot_w = dt_sb[:, 0:NB * SLOT].rearrange("p (b s) -> p b s", b=NB)
        b1_sb = dt_sb[:, 256:256 + NE * MCH].rearrange("p (e c) -> p e c", e=NE)
        b2_sb = dt_sb[:, 384:384 + NE * DCH].rearrange("p (e c) -> p e c", e=NE)
        round_v = hbuf[:].rearrange("p (a h) -> p a h", h=D)
        wv_sb = hbuf[:].rearrange("p (c n) -> p c n", c=CCH)
        hid = hbuf[:].rearrange("p (m s) -> p m s", m=MCH)
        round_g = small[:].rearrange("p (a h) -> p a h", h=D)
        k_time = small[:, 0:D]
        x_win = small[:, 0:256].rearrange("p (c s) -> p c s", c=DCH)
        y_win = small[:, 256:512].rearrange("p (c s) -> p c s", c=DCH)
        y_out = small[0:SLOT, 512:1024]
        y_tok = xn2

        _next = [0]

        def col(n):
            _next[0] += n
            assert _next[0] <= COLS
            return cols[:, _next[0] - n:_next[0]]

        lam_c, decay = col(2), col(1)
        step_mag, step_ph = col(AH + BL), col(AH + BL)
        bn6, mv = col(6), col(2 * NB)
        rstd, var_eps, m_half = col(NB), col(NB), col(NB)
        bkq_sb = col(2 * DCH).rearrange("p (e k) -> p e k", k=2)
        bkq_prod, bkq_sum = col(DCH), col(1)
        qbias, wqb, q_bk = col(3), col(DCH), col(NB)
        qmax, rsum, nbias = col(NB * NQ), col(NB * NQ), col(NB)
        rmax, rmax_q, rtot, spare = col(1), col(1), col(1), col(5)
        logits = tab[:, TABLES["pick"][0]:TABLES["pick"][0] + NB * NE].rearrange("p (b e) -> p b e", e=NE)
        rt0 = TABLES["cos_f"][0]

        def route(i, n):
            return tab[:, rt0 + i:rt0 + i + n]

        lmax = route(0, 4)
        lsub = route(4, 32).rearrange("p (b e) -> p b e", e=NE)
        first = route(36, 32).rearrange("p (b e) -> p b e", e=NE)
        hot = route(68, 32).rearrange("p (b e) -> p b e", e=NE)
        fmax = route(100, 4)
        psum_e, prob = route(104, 4), route(108, 4)
        rt1 = TABLES["sin_f"][0]
        lexp = tab[:, rt1:rt1 + 32].rearrange("p (b e) -> p b e", e=NE)
        nwin = tab[:, rt1 + 32:rt1 + 40]
        cum9 = tab[:, rt1 + 40:rt1 + 49]
        base = tab[:, rt1 + 49:rt1 + 57]
        slot_e = tab[:, rt1 + 57:rt1 + 89].rearrange("p (b e) -> p b e", e=NE)
        slot = tab[:, rt1 + 89:rt1 + 93]
        slot64 = tab[:, rt1 + 93:rt1 + 97]
        rt2 = TABLES["cos_t"][0]
        cum_prod = tab[:, rt2:rt2 + 72].rearrange("p (e f) -> p e f", f=NE)
        iota_w = table("iota")
        win_i = icols[:, 0:NE + 1]
        row_i = icols[:, 9:13].bitcast(U32)
        wg_sb = sb("wg_sb", [P, DCH, NE])
        bg_sb = sb("bg_sb", [P, NE])
        d_sb = kfreq[0:1, 1, :]

        filled = [sem(f"bank{k}_filled") for k in range(8)]
        drained = [sem(f"bank{k}_drained") for k in range(8)]
        place_loaded = [sem(f"place{k}_loaded") for k in range(NSLOT)]
        params_loaded, tab_loaded, x_loaded = sem("params_loaded"), sem("tab_loaded"), sem("x_loaded")
        qk_loaded, bv_loaded, wri_loaded = sem("qk_loaded"), sem("bv_loaded"), sem("wri_loaded")
        wv_loaded, gate_loaded, d_loaded = sem("wv_loaded"), sem("gate_loaded"), sem("d_loaded")
        bias_loaded = sem("bias_loaded")
        dve_step = sem("dve_step")
        pool_step = sem("pool_step")
        dt_ready, step_mag_ready, step_ph_ready = sem("dt_ready"), sem("step_mag_ready"), sem("step_ph_ready")
        half_ready, zeros_ready, mags_ready = sem("half_ready"), sem("zeros_ready"), sem("mags_ready")
        a_phase_ready, b_phase_ready = sem("a_phase_ready"), sem("b_phase_ready")
        a_sin_ready, b_sin_ready, wr_done = sem("a_sin_ready"), sem("b_sin_ready"), sem("wr_done")
        a_tab_ready, b_tab_ready = sem("a_tab_ready"), sem("b_tab_ready")
        var_ready, rstd_ready = sem("var_ready"), sem("rstd_ready")
        xn1_ready, bkq_ready, rmax_ready = sem("xn1_ready"), sem("bkq_ready"), sem("rmax_ready")
        u_ready, spec_ready, xn2_ready = sem("u_ready"), sem("spec_ready"), sem("xn2_ready")
        hot_ready, lsub_ready, lexp_ready = sem("hot_ready"), sem("lsub_ready"), sem("lexp_ready")
        windows_ready, rows_ready = sem("windows_ready"), sem("rows_ready")
        onehot_ready, iota_ready = sem("onehot_ready"), sem("iota_ready")
        xw_filled, xw_ready = sem("xw_filled"), sem("xw_ready")
        ha_filled, hb_filled, ha_ready, hb_ready = sem("ha_filled"), sem("hb_filled"), sem("ha_ready"), sem("hb_ready")
        ya_done, y_filled, y_ready = sem("ya_done"), sem("y_filled"), sem("y_ready")
        yt_filled, rows_out_ready, rows_sent = sem("yt_filled"), sem("rows_out_ready"), sem("rows_sent")
        gathered = [sem(f"gathered{b}") for b in range(NB)]
        result_ready, result_sent = sem("result_ready"), sem("result_sent")

        def weight_place(j):
            return (4, 5, 6, 7, 0, 1, 2, 3, 8, 9)[j % NSLOT]

        def weight_count(j):
            return j // NSLOT + (2 if weight_place(j) < NB else 1)

        def after_fill(eng, what):
            b, n = FILL_NO[what]
            eng.wait_ge(filled[b], n)

        def after_read(eng, what):
            b, n = FILL_NO[what]
            eng.wait_ge(drained[b], n)

        def may_fill(eng, what):
            b, n = FILL_NO[what]
            if n > 1:
                eng.wait_ge(drained[b], n - 1)
            return bank[:, b, :]

        def did_fill(ins, what):
            ins.then_inc(filled[FILL_NO[what][0]], 1)

        def may_read(eng, what):
            after_fill(eng, what)
            return bank[:, FILL_NO[what][0], :]

        def did_read(ins, what):
            ins.then_inc(drained[FILL_NO[what][0]], 1)

        block = stack.enter_context(nc.Block())

        @block.sync
        def _(sp):
            sp.dma_start(x_sb[:], x_rows).then_inc(x_loaded, 16)
            sp.dma_start(wk_sb, wk_t.rearrange("(e p) c -> p e c", p=P)).then_inc(qk_loaded, 16)
            sp.dma_start(wq_sb, wq_t.rearrange("(e p) d -> p e d", p=P)).then_inc(qk_loaded, 16)
            for b in range(NB):
                if b == 2:
                    sp.wait_ge(a_tab_ready, 1)
                sp.dma_start(ring[:, b, :], ctx[b].rearrange("(p k) c -> p (k c)", p=P)) \
                    .then_inc(place_loaded[b], 16)
            sp.dma_start(wv_sb, wv.rearrange("(c p) n -> p c n", p=P)).then_inc(wv_loaded, 16)

            def load_unit(j):
                e, u = divmod(j, UNITS)
                place = ring[:, weight_place(j), :]
                if u < 2:
                    src = w1[e].rearrange("(d p) m -> p d m", p=P)[:, :, u * 1024:(u + 1) * 1024]
                    dst = place.rearrange("p (d m) -> p d m", d=DCH)
                else:
                    src = w2[e].rearrange("(m p) n -> p m n", p=P)[:, (u - 2) * 8:(u - 1) * 8, :]
                    dst = place.rearrange("p (m n) -> p m n", m=8)
                sp.dma_start(dst, src).then_inc(place_loaded[weight_place(j)], 16)

            for j in range(NSLOT):
                if j == 0:
                    after_fill(sp, ("k1", 7))
                if j == 1:
                    after_fill(sp, ("k2",))
                if 4 <= j < 8:
                    after_fill(sp, ("pv", j - 4))
                load_unit(j)
            sp.wait_ge(windows_ready, 1)
            last = [sp.value_load(win_i[0:1, e + 1:e + 2], min_val=0, max_val=MAXW) for e in range(NE)]
            for j in range(NSLOT, NE * UNITS):
                e, u = divmod(j - NSLOT, UNITS)
                sp.wait_ge((ha_filled, hb_filled, ya_done, y_filled)[u], last[e] + 1)
                sp.wait_ge(place_loaded[weight_place(j)], 16 * (weight_count(j) - 1))
                load_unit(j)
            for b in range(NB):
                sp.wait_ge(result_ready, b + 1)
                sp.dma_start(out_rows[:, b, :], x_sb[:, b, :]).then_inc(result_sent, 16)
            sp.wait_ge(result_sent, 16 * NB)
            sp.dma_start(cols[:, 0:2], lam).then_inc(params_loaded, 16)
            sp.wait_ge(params_loaded, 48)

        @block.scalar
        def _(act):
            act.dma_start(lam_c, lam).then_inc(params_loaded, 16)
            act.dma_start(dt_sb[:], log_dt.partition_broadcast(P)).then_inc(params_loaded, 16)
            act.dma_start(tab[:], tables).then_inc(tab_loaded, 16)
            act.dma_start(bv_sb, bv.partition_broadcast(P)).then_inc(bv_loaded, 16)
            act.dma_start(bkq_sb, bkq.rearrange("(e p) k -> p e k", p=P)).then_inc(qk_loaded, 16)
            act.dma_start(wri[:], w_ri.rearrange("k n h -> n k h")).then_inc(wri_loaded, 16)
            act.dma_start(wg_sb[:], w_gate.rearrange("(c p) e -> p c e", p=P)).then_inc(gate_loaded, 16)
            act.dma_start(bg_sb[:], b_gate.partition_broadcast(P)).then_inc(gate_loaded, 16)
            act.dma_start(d_sb, d_skip).then_inc(d_loaded, 16)

            act.wait_ge(params_loaded, 32)
            act.activation(decay, lam_c[:, 0:1], ACT.Exp).then_inc(dt_ready, 1)
            act.activation(dt_sb[:], dt_sb[:], ACT.Exp).then_inc(dt_ready, 1)

            act.wait_ge(dt_ready, 2)
            act.wait_ge(step_mag_ready, 1)
            for i in range(AH + BL):
                dst = a_tab[:, i, :] if i < AH else b_tab[:, i - AH, :]
                ins = act.activation(dst, dt_sb[:], ACT.Exp, scale=step_mag[:, i:i + 1])
            ins.then_inc(mags_ready, 1)

            after_read(act, ("bias",))
            for c in range(CCH):
                src = may_read(act, ("q", c))
                did_read(act.activation(q_t[:, c, :], src, ACT.Identity, bias=qbias[:, c:c + 1]), ("q", c))

            for i in range(4):
                act.wait_ge(a_phase_ready, 2 * i + 2)
                sines = a_sin[:, 4 * i:4 * i + 4, :]
                act.activation(sines, sines, ACT.Sin, scale=-TWO_PI).then_inc(a_sin_ready, 1)
            for i in range(4):
                act.wait_ge(b_phase_ready, 2 * i + 2)
                sines = (b_sin1, b_sin2)[i // 2][:, 4 * (i % 2):4 * (i % 2) + 4, :]
                act.activation(sines, sines, ACT.Sin, scale=-TWO_PI).then_inc(b_sin_ready, 1)

            def softmax_exp(b):
                act.wait_ge(rmax_ready, b + 1)
                for j in range(NQ):
                    if b > 0:
                        after_fill(act, ("pT", b - 1, j))
                    src = may_read(act, ("s", b, j))
                    did_read(act.activation(probs[:, j * 512:(j + 1) * 512], src, ACT.Exp,
                                            bias=nbias[:, b:b + 1], accum_out=rsum[:, NQ * b + j:NQ * b + j + 1]),
                             ("s", b, j))

            def turned_gate_rows(b):
                src = may_read(act, ("x2T", b))
                if b > 0:
                    after_fill(act, ("lg", b - 1))
                did_read(act.activation(xn2_t, src.rearrange("p (c n) -> p c n", c=DCH), ACT.Identity), ("x2T", b))

            softmax_exp(0)
            for b in range(NB):
                for j in range(NQ):
                    if j % 2:
                        src = may_read(act, ("pT", b, j))
                        if b > 0:
                            after_fill(act, ("pv", b - 1))
                        did_read(act.activation(probs_t[:, KPQ * j:KPQ * j + KPQ, :],
                                                src.rearrange("p (k n) -> p k n", k=KPQ), ACT.Identity),
                                 ("pT", b, j))
                    if b + 1 < NB:
                        src = may_read(act, ("ct", b + 1, j, 1))
                        after_fill(act, ("s", b + 1, j - 2) if j >= 2 else ("s", b, j + 2))
                        did_read(act.activation(ctx_t[:, j % 2, 1, :], src, ACT.Identity), ("ct", b + 1, j, 1))
                if b + 1 < NB:
                    softmax_exp(b + 1)
                if b >= 2:
                    turned_gate_rows(b - 2)
            turned_gate_rows(2)
            turned_gate_rows(3)
            after_read(act, ("av", 3))
            act.dma_start(b1_sb, b1).then_inc(bias_loaded, 16)
            act.dma_start(b2_sb, b2).then_inc(bias_loaded, 16)
            act.wait_ge(lsub_ready, 1)
            act.activation(lexp, lsub, ACT.Exp).then_inc(lexp_ready, 1)

            act.wait_ge(bias_loaded, 32)
            act.wait_ge(windows_ready, 1)
            bounds = [act.value_load(win_i[0:1, e:e + 1], min_val=0, max_val=MAXW) for e in range(NE + 1)]

            def rows_out(w):
                act.wait_ge(yt_filled, w + 1)
                act.wait_ge(rows_sent, 16 * w + 16)
                act.activation(y_out, bank[0:SLOT, YT, :], ACT.Identity).then_inc(rows_out_ready, 1)

            for e in range(NE):
                with act.If(bounds[e] < bounds[e + 1]):
                    with act.Fori(bounds[e], bounds[e + 1]) as w:
                        act.wait_ge(ha_filled, w + 2)
                        for m in range(8):
                            ins = act.activation(hid[:, m, :], bank[:, HA, m * SLOT:(m + 1) * SLOT], ACT.Relu,
                                                 bias=b1_sb[:, e, m:m + 1])
                        ins.then_inc(ha_ready, 1)
                        rows_out(w)
                        act.wait_ge(y_filled, w + 2)
                        for c in range(DCH):
                            ins = act.activation(y_win[:, c, :], bank[:, YB, c * SLOT:(c + 1) * SLOT],
                                                 ACT.Identity, bias=b2_sb[:, e, c:c + 1])
                        ins.then_inc(y_ready, 1)
            rows_out(bounds[NE])

        @block.vector
        def _(dve):
            steps = [0]

            def link(ins):
                steps[0] += 1
                ins.then_inc(dve_step, 1)
                dve.wait_ge(dve_step, steps[0])

            dve.memset(m_half, -0.5).then_inc(half_ready, 1)
            dve.wait_ge(tab_loaded, 16)
            dve.wait_ge(dt_ready, 2)
            dve.tensor_scalar(step_mag, table("steps"), decay, -1.0, ALU.mult, ALU.mult).then_inc(step_mag_ready, 1)
            dve.tensor_scalar(step_ph, table("steps"), lam_c[:, 1:2], 1.0 / TWO_PI, ALU.mult, ALU.mult) \
                .then_inc(step_ph_ready, 1)

            norms = [0]

            def layer_norm(tiles, dst):
                n = len(tiles)
                for i, t in enumerate(tiles):
                    link(dve.bn_stats(bn6, x_sb[:, t, :]))
                    link(dve.bn_aggr(mv[:, 2 * i:2 * i + 2], bn6))
                var = mv.rearrange("p (t k) -> p t k", k=2)[:, 0:n, 1:2]
                dve.tensor_scalar(var_eps[:, 0:n].unsqueeze(2), var, EPS, None, ALU.add).then_inc(var_ready, 1)
                norms[0] += 1
                dve.wait_ge(rstd_ready, norms[0])
                for i, t in enumerate(tiles):
                    ins = dve.tensor_scalar(dst[i], x_sb[:, t, :], mv[:, 2 * i:2 * i + 1], rstd[:, i:i + 1],
                                            ALU.subtract, ALU.mult)
                return ins

            dve.wait_ge(x_loaded, 16)
            layer_norm(range(NB), [xn1[:, b, :] for b in range(NB)]).then_inc(xn1_ready, 1)

            dve.wait_ge(qk_loaded, 48)
            link(dve.tensor_tensor(bkq_prod, bkq_sb[:, :, 0], bkq_sb[:, :, 1], ALU.mult))
            dve.tensor_reduce(bkq_sum, bkq_prod, AX, ALU.add).then_inc(bkq_ready, 1)
            for d in range(DCH):
                src = may_read(dve, ("wqk", d))
                dve.tensor_copy(wqk[:, d, :], src[:, 0:DC])
                did_read(dve.tensor_copy(wqb[:, d:d + 1], src[:, DC:DC + 1]), ("wqk", d))
            src = may_read(dve, ("bias",))
            did_read(dve.tensor_copy(qbias, src[:, 0:3]), ("bias",))
            for b in range(NB):
                src = may_read(dve, ("xnT", b))
                did_read(dve.tensor_copy(xn1_t[:, :, b * P:(b + 1) * P], src.rearrange("p (c n) -> p c n", c=DCH)),
                         ("xnT", b))
            dve.wait_ge(xn1_ready, 1)
            dve.wait_ge(bv_loaded, 16)
            link(dve.tensor_tensor(x_sb[:], x_sb[:], bv_sb.unsqueeze(1).to_broadcast([P, NB, D]), ALU.add))
            src = may_read(dve, ("qb",))
            after_read(dve, ("bias",))
            did_read(dve.tensor_scalar(q_bk, src[:, 0:NB], qbias[:, 2:3], None, ALU.add), ("qb",))

            dve.wait_ge(step_ph_ready, 1)
            for i in range(AH // 2):
                turns = a_sin[:, 2 * i:2 * i + 2, :]
                for a in (2 * i, 2 * i + 1):
                    ins = dve.tensor_scalar(a_sin[:, a, :], dt_sb[:], step_ph[:, a:a + 1], table("phase")[:, 0:1],
                                            ALU.mult, ALU.add)
                link(ins)
                link(dve.tensor_scalar(round_v, turns, ROUND, None, ALU.add))
                dve.scalar_tensor_tensor(out=turns, in0=round_v, scalar=ROUND, in1=turns, op0=ALU.subtract,
                                         op1=ALU.subtract).then_inc(a_phase_ready, 1)

            def context_read(b, j):
                for c in range(CCH if b == 0 else 1):
                    src = may_read(dve, ("ct", b, j, c))
                    if j >= 2:
                        after_fill(dve, ("s", b, j - 2))
                    elif b > 0:
                        after_fill(dve, ("s", b - 1, j + 2))
                    did_read(dve.tensor_copy(ctx_t[:, j % 2, c, :], src), ("ct", b, j, c))

            def quarter_max(b, j):
                src = may_read(dve, ("s", b, j))
                return dve.tensor_reduce(qmax[:, NQ * b + j:NQ * b + j + 1], src, AX, ALU.max)

            def row_bias(b):
                link(dve.tensor_reduce(rmax, qmax[:, NQ * b:NQ * b + NQ], AX, ALU.max))
                link(dve.tensor_tensor(rmax_q, rmax, q_bk[:, b:b + 1], ALU.add))
                dve.tensor_tensor(nbias[:, b:b + 1], q_bk[:, b:b + 1], rmax_q, ALU.subtract).then_inc(rmax_ready, 1)

            for j in range(NQ):
                context_read(0, j)
                if j > 0:
                    quarter_max(0, j - 1)
            link(quarter_max(0, NQ - 1))
            row_bias(0)
            dve.wait_ge(mags_ready, 1)
            for i in range(4):
                dve.wait_ge(a_sin_ready, i + 1)
                rows = slice(4 * i, 4 * i + 4)
                ins = dve.tensor_tensor(a_tab[:, rows, :], a_tab[:, rows, :], a_sin[:, rows, :], ALU.mult)
            ins.then_inc(a_tab_ready, 1)

            def b_table():
                dve.wait_ge(b_sin_ready, 4)
                dve.wait_ge(wri_loaded, 16)
                link(dve.tensor_tensor(b_sin2, b_sin2, wri[:, 1, :].unsqueeze(1).to_broadcast([P, BL, D]), ALU.mult))
                dve.wait_ge(wr_done, 1)
                link(dve.tensor_tensor(b_sin1, b_sin1, b_sin2, ALU.add))
                dve.tensor_tensor(b_tab, b_tab, b_sin1, ALU.mult).then_inc(b_tab_ready, 1)

            def kernel_reads():
                own = table("own").unsqueeze(1).unsqueeze(1).to_broadcast([P, 8, BL, HG])
                for g in range(8):
                    src = may_read(dve, ("k1", g)).rearrange("p (g b h) -> p g b h", g=8, b=BL)
                    if g == 0:
                        dve.wait_ge(b_tab_ready, 1)
                    dst = k_parts.rearrange("p b (h g) -> p g b h", h=HG)[:, 8 * g:8 * g + 8, :, :]
                    did_read(dve.tensor_tensor(dst, src, own, ALU.mult), ("k1", g))
                src = may_read(dve, ("k2",))
                dve.wait_ge(b_phase_ready, 8)
                link(dve.tensor_copy(k_time, src))
                dve.wait_ge(d_loaded, 16)
                did_read(dve.tensor_tensor(k_time[0:1, :], k_time[0:1, :], d_sb, ALU.add), ("k2",))
                for i in range(2):
                    src = may_read(dve, ("k3", i))
                    did_read(dve.tensor_copy(kfreq[:, i, :], src), ("k3", i))

            def attention_out(b):
                src = may_read(dve, ("pv", b))
                link(dve.tensor_reduce(rtot, rsum[:, NQ * b:NQ * b + NQ], AX, ALU.add))
                link(dve.reciprocal(rtot, rtot))
                if b == 0:
                    dve.wait_ge(b_phase_ready, 8)
                did_read(dve.tensor_scalar(an, src[:, 0:DC], rtot, None, ALU.mult), ("pv", b))

            def value_reads(b):
                src = may_read(dve, ("anT", b))
                did_read(dve.tensor_copy(an_t, src[:, 0:DC].rearrange("p (c n) -> p c n", c=CCH)), ("anT", b))
                src = may_read(dve, ("av", b))
                did_read(dve.tensor_tensor(x_sb[:, b, :], src, x_sb[:, b, :], ALU.add), ("av", b))
                after_read(dve, ("av", b))
                if b == 0:
                    dve.wait_ge(wr_done, 1)
                layer_norm([b], [u_sb]).then_inc(u_ready, 1)

            def freq_reads(b):
                uc, us = may_read(dve, ("uc", b)), may_read(dve, ("us", b))
                kc, ks = kfreq[:, 0, :], kfreq[:, 1, :]
                dve.tensor_tensor(prod1, uc, ks, ALU.mult)
                did_read(dve.tensor_tensor(y_cos, uc, kc, ALU.mult), ("uc", b))
                dve.tensor_tensor(prod2, us, ks, ALU.mult)
                did_read(dve.tensor_tensor(y_sin, us, kc, ALU.mult), ("us", b))
                after_read(dve, ("us", b))
                dve.tensor_tensor(y_cos, y_cos, prod2, ALU.subtract)
                dve.tensor_tensor(y_sin, y_sin, prod1, ALU.add).then_inc(spec_ready, 1)

            def time_reads(b):
                src = may_read(dve, ("y", b))
                did_read(dve.tensor_tensor(x_sb[:, b, :], src, x_sb[:, b, :], ALU.add), ("y", b))
                after_read(dve, ("y", b))
                layer_norm([b], [xn2[:, b, :]]).then_inc(xn2_ready, 1)

            def gate_reads(b):
                dve.wait_ge(gate_loaded, 32)
                src = may_read(dve, ("lg", b))
                did_read(dve.tensor_tensor(logits[:, b, :], src[:, 0:NE], bg_sb[:], ALU.add), ("lg", b))

            for b in range(NB):
                for j in range(NQ):
                    if j % 2 == 0:
                        src = may_read(dve, ("pT", b, j))
                        if b > 0:
                            after_fill(dve, ("pv", b - 1))
                        did_read(dve.tensor_copy(probs_t[:, KPQ * j:KPQ * j + KPQ, :],
                                                 src.rearrange("p (k n) -> p k n", k=KPQ)), ("pT", b, j))
                    if b + 1 < NB:
                        context_read(b + 1, j)
                        ins = quarter_max(b + 1, j)
                if b + 1 < NB:
                    link(ins)
                    row_bias(b + 1)
                if b == 0:
                    b_table()
                if b == 1:
                    kernel_reads()
                if b >= 1:
                    value_reads(b - 1)
                if b >= 2:
                    time_reads(b - 2)
                attention_out(b)
                if b >= 1:
                    freq_reads(b - 1)
                if b >= 2:
                    gate_reads(b - 2)
            value_reads(3)
            time_reads(2)
            freq_reads(3)
            gate_reads(2)
            time_reads(3)
            gate_reads(3)

            def per_e(v):
                return v.unsqueeze(2).to_broadcast([P, NB, NE])

            after_read(dve, ("lg", 3))
            link(dve.tensor_reduce(lmax, logits, AX, ALU.max))
            link(dve.tensor_tensor(first, logits, per_e(lmax), ALU.is_equal))
            link(dve.tensor_tensor(first, first, table("rank_e").unsqueeze(1).to_broadcast([P, NB, NE]), ALU.mult))
            link(dve.tensor_reduce(fmax, first, AX, ALU.max))
            dve.tensor_tensor(hot, first, per_e(fmax), ALU.is_equal).then_inc(hot_ready, 1)
            dve.tensor_tensor(lsub, logits, per_e(lmax), ALU.subtract).then_inc(lsub_ready, 1)

            src = may_read(dve, ("route",))
            ranks = src[:, 0:NB * NE].rearrange("p (b e) -> p b e", e=NE)
            counts = src[:, NB * NE:NB * NE + NE]
            link(dve.tensor_scalar(nwin, counts, SLOT / 2 - 0.5, 1.0 / SLOT, ALU.add, ALU.mult))
            link(dve.tensor_scalar(nwin, nwin, ROUND, None, ALU.add))
            link(dve.tensor_scalar(nwin, nwin, ROUND, None, ALU.subtract))
            before = table("before_e").rearrange("p (e f) -> p e f", f=NE)
            link(dve.tensor_tensor(cum_prod, before, nwin.unsqueeze(1).to_broadcast([P, NE + 1, NE]), ALU.mult))
            link(dve.tensor_reduce(cum9, cum_prod, AX, ALU.add))
            dve.tensor_copy(win_i, cum9).then_inc(windows_ready, 1)
            link(dve.tensor_scalar(base, cum9[:, 0:NE], float(SLOT), None, ALU.mult))
            link(dve.tensor_tensor(slot_e, ranks, base.unsqueeze(1).to_broadcast([P, NB, NE]), ALU.add))
            link(dve.tensor_tensor(slot_e, slot_e, hot, ALU.mult))
            link(dve.tensor_reduce(slot, slot_e, AX, ALU.add))

            dve.memset(y_win, 0.0).then_inc(y_ready, 1)
            for i, s in enumerate((ha_filled, hb_filled, ya_done, y_filled, rows_out_ready)):
                dve.memset(spare[:, i:i + 1], 0.0).then_inc(s, 1)

            def onehot_columns(n):
                dve.tensor_tensor(onehot_w, iota_w.unsqueeze(1).to_broadcast([P, NB, SLOT]),
                                  slot.unsqueeze(2).to_broadcast([P, NB, SLOT]), ALU.is_equal).then_inc(onehot_ready, 1)
                dve.wait_ge(onehot_ready, n)
                dve.tensor_scalar(iota_w, iota_w, float(SLOT), None, ALU.add).then_inc(iota_ready, 1)

            onehot_columns(1)
            link(dve.tensor_scalar(slot64, slot, float(SLOT), None, ALU.add))
            dve.tensor_copy(row_i, slot64).then_inc(rows_ready, 1)
            dve.wait_ge(lexp_ready, 1)
            link(dve.tensor_reduce(psum_e, lexp, AX, ALU.add))
            link(dve.reciprocal(prob, psum_e))

            def window_rows(n):
                dve.wait_ge(xw_filled, n)
                dve.tensor_copy(x_win, bank[:, XW, 0:DCH * SLOT].rearrange("p (c s) -> p c s", c=DCH)) \
                    .then_inc(xw_ready, 1)

            window_rows(1)
            dve.wait_ge(windows_ready, 1)
            bounds = [dve.value_load(win_i[0:1, e:e + 1], min_val=0, max_val=MAXW) for e in range(NE + 1)]
            dve.wait_ge(bias_loaded, 32)
            for e in range(NE):
                with dve.If(bounds[e] < bounds[e + 1]):
                    with dve.Fori(bounds[e], bounds[e + 1]) as w:
                        dve.wait_ge(xw_filled, w + 1)
                        dve.wait_ge(iota_ready, w + 1)
                        onehot_columns(w + 2)
                        dve.wait_ge(hb_filled, w + 2)
                        for m in range(8):
                            ins = dve.tensor_scalar(hid[:, 8 + m, :], bank[:, HB, m * SLOT:(m + 1) * SLOT],
                                                    b1_sb[:, e, 8 + m:9 + m], 0.0, ALU.add, ALU.max)
                        ins.then_inc(hb_ready, 1)
                        window_rows(w + 2)

            for b in range(NB):
                dve.wait_ge(gathered[b], 16)
                dve.scalar_tensor_tensor(out=x_sb[:, b, :], in0=y_tok[:, b, :], scalar=prob[:, b:b + 1],
                                         in1=x_sb[:, b, :], op0=ALU.mult, op1=ALU.add).then_inc(result_ready, 1)

        @block.gpsimd
        def _(pool):
            steps = [0]

            def link(ins):
                steps[0] += 1
                ins.then_inc(pool_step, 1)
                pool.wait_ge(pool_step, steps[0])

            def inverse_root(k):
                pool.wait_ge(var_ready, k)
                pool.tensor_tensor(rstd, var_eps, m_half, ALU.pow).then_inc(rstd_ready, 1)

            pool.wait_ge(half_ready, 1)
            inverse_root(1)
            pool.wait_ge(tab_loaded, 16)
            pool.wait_ge(dt_ready, 2)
            pool.wait_ge(step_ph_ready, 1)
            for i in range(2 * BL // 2):
                dst, r = (b_sin1, b_sin2)[i // 4], 2 * (i % 4)
                turns = dst[:, r:r + 2, :]
                for k in (r, r + 1):
                    ins = pool.tensor_scalar(dst[:, k, :], dt_sb[:], step_ph[:, AH + k:AH + k + 1],
                                             table("phase")[:, 1 + i // 4:2 + i // 4], ALU.mult, ALU.add)
                link(ins)
                link(pool.tensor_scalar(round_g, turns, ROUND, 1.0, ALU.add, ALU.mult))
                link(pool.tensor_scalar(round_g, round_g, -ROUND, 1.0, ALU.add, ALU.mult))
                pool.tensor_tensor(turns, round_g, turns, ALU.subtract).then_inc(b_phase_ready, 1)
            pool.wait_ge(b_phase_ready, 2 * BL // 2)
            pool.memset(y_out, 0.0).then_inc(zeros_ready, 1)
            pool.wait_ge(zeros_ready, 1)
            pool.dma_start(y_rows[(MINW + 1) * SLOT:, :].rearrange("(w s) n -> s w n", s=SLOT),
                           y_out.unsqueeze(1).to_broadcast([SLOT, MAXW - MINW, D])).then_inc(rows_sent, 16)
            pool.wait_ge(b_sin_ready, 2)
            pool.wait_ge(wri_loaded, 16)
            pool.tensor_tensor(b_sin1, b_sin1, wri[:, 0, :].unsqueeze(1).to_broadcast([P, BL, D]), ALU.mult) \
                .then_inc(wr_done, 1)
            for k in range(2 * NB):
                inverse_root(k + 2)

            pool.wait_ge(windows_ready, 1)
            n_windows = pool.value_load(win_i[0:1, NE:NE + 1], min_val=0, max_val=MAXW)
            with pool.Fori(0, n_windows + 1) as w:
                pool.wait_ge(rows_out_ready, w + 2)
                pool.dma_start(y_rows[bass.ds(w * SLOT, SLOT), :], y_out).then_inc(rows_sent, 16)
            pool.wait_ge(xw_filled, n_windows + 1)
            pool.wait_ge(rows_sent, 16 * n_windows + 32)
            pool.tensor_tensor(rstd, m_half, m_half, ALU.mult)
            pool.wait_ge(rows_ready, 1)
            for b in range(NB):
                pool.indirect_dma_start(y_tok[:, b, :], None, y_rows,
                                        bass.IndirectOffsetOnAxis(ap=row_i[:, b:b + 1], axis=0)) \
                    .then_inc(gathered[b], 16)

        @block.tensor
        def _(pe):
            def col_slice(c):
                return slice(c * P, (c + 1) * P)

            pe.wait_ge(qk_loaded, 48)
            for d in range(DCH):
                dst = may_fill(pe, ("wqk", d))
                for e in range(DCH):
                    pe.matmul(dst[:, 0:DC], wq_sb[:, e, col_slice(d)], wk_sb[:, e, :], start=e == 0, stop=e == DCH - 1)
                for e in range(DCH):
                    ins = pe.matmul(dst[:, DC:DC + 1], wq_sb[:, e, col_slice(d)], bkq_sb[:, e, 0:1],
                                    start=e == 0, stop=e == DCH - 1)
                did_fill(ins, ("wqk", d))
            dst = may_fill(pe, ("bias",))
            for c in range(CCH):
                for e in range(DCH):
                    pe.matmul(dst[:, c:c + 1], wk_sb[:, e, col_slice(c)], bkq_sb[:, e, 1:2],
                              start=e == 0, stop=e == DCH - 1)
            pe.wait_ge(tab_loaded, 16)
            pe.wait_ge(bkq_ready, 1)
            did_fill(pe.matmul(dst[:, 2:3], ones, bkq_sum, start=True, stop=True), ("bias",))
            pe.wait_ge(xn1_ready, 1)
            for b in range(NB):
                dst = may_fill(pe, ("xnT", b))
                for c in range(DCH):
                    ins = pe.transpose(dst[:, col_slice(c)], xn1[:, b, col_slice(c)], ident)
                did_fill(ins, ("xnT", b))
            for d in range(DCH):
                after_read(pe, ("wqk", d))
            for b in range(NB):
                after_read(pe, ("xnT", b))
            for c in range(CCH):
                dst = may_fill(pe, ("q", c))
                for d in range(DCH):
                    ins = pe.matmul(dst, wqk[:, d, col_slice(c)], xn1_t[:, d, :], start=d == 0, stop=d == DCH - 1)
                did_fill(ins, ("q", c))
            dst = may_fill(pe, ("qb",))
            for b in range(NB):
                for d in range(DCH):
                    ins = pe.matmul(dst[:, b:b + 1], xn1_t[:, d, col_slice(b)], wqb[:, d:d + 1],
                                    start=d == 0, stop=d == DCH - 1)
            did_fill(ins, ("qb",))

            def turn_context(b, j):
                if j == 0:
                    pe.wait_ge(place_loaded[b], 16)
                for c in range(CCH):
                    dst = may_fill(pe, ("ct", b, j, c))
                    for k in range(KPQ):
                        ins = pe.transpose(dst[:, col_slice(k)], ctx_sb[b][:, KPQ * j + k, col_slice(c)], ident)
                    did_fill(ins, ("ct", b, j, c))

            def scores(b, j):
                dst = may_fill(pe, ("s", b, j))
                for c in range(CCH):
                    if b == 0 and j == 0:
                        after_read(pe, ("q", c))
                    after_read(pe, ("ct", b, j, c))
                    ins = pe.matmul(dst, q_t[:, c, col_slice(b)], ctx_t[:, j % 2, c, :], start=c == 0, stop=c == CCH - 1)
                did_fill(ins, ("s", b, j))

            def turn_probs(b, j):
                after_read(pe, ("s", b, j))
                dst = may_fill(pe, ("pT", b, j))
                for k in range(KPQ):
                    ins = pe.transpose(dst[:, col_slice(k)], probs[:, col_slice(KPQ * j + k)], ident)
                did_fill(ins, ("pT", b, j))

            def probs_context(b):
                dst = may_fill(pe, ("pv", b))
                for j in range(NQ):
                    after_read(pe, ("pT", b, j))
                    for k in range(KPQ * j, KPQ * j + KPQ):
                        ins = pe.matmul(dst[:, 0:DC], probs_t[:, k, :], ctx_sb[b][:, k, :],
                                        start=k == 0, stop=k == KCH - 1)
                did_fill(ins, ("pv", b))

            def kernel_products():
                pe.wait_ge(a_tab_ready, 1)
                pe.wait_ge(b_tab_ready, 1)
                a_cols = a_tab.rearrange("p a (h g) -> p (a h) g", h=HG)
                b_cols = b_tab.rearrange("p b (h g) -> p (b h) g", h=HG)
                for g in range(8):
                    dst = may_fill(pe, ("k1", g))
                    for i in range(8):
                        ins = pe.matmul(dst[:, i * BL * HG:(i + 1) * BL * HG], a_cols[:, :, 8 * g + i],
                                        b_cols[:, :, 8 * g + i], start=True, stop=True)
                    did_fill(ins, ("k1", g))
                dst = may_fill(pe, ("k2",))
                after_read(pe, ("k1", 6))
                after_read(pe, ("k1", 7))
                pick = table("pick")
                for i in range(BL):
                    ins = pe.matmul(dst, pick[:, BL - 1 - i:BL - 1 - i + P], k_parts[:, i, :],
                                    start=i == 0, stop=i == BL - 1)
                did_fill(ins, ("k2",))
                after_read(pe, ("k2",))
                for i in range(2):
                    dst = may_fill(pe, ("k3", i))
                    did_fill(pe.matmul(dst, table(("cos_f", "sin_f")[i]), k_time, start=True, stop=True), ("k3", i))

            def values(b):
                dst = may_fill(pe, ("anT", b))
                after_read(pe, ("pv", b))
                for c in range(CCH):
                    ins = pe.transpose(dst[:, col_slice(c)], an[:, col_slice(c)], ident)
                did_fill(ins, ("anT", b))
                dst = may_fill(pe, ("av", b))
                pe.wait_ge(wv_loaded, 16)
                after_read(pe, ("anT", b))
                for c in range(CCH):
                    ins = pe.matmul(dst, an_t[:, c, :], wv_sb[:, c, :], start=c == 0, stop=c == CCH - 1)
                did_fill(ins, ("av", b))

            def to_frequency(b):
                pe.wait_ge(u_ready, b + 1)
                for what, name in ((("uc", b), "cos_f"), (("us", b), "sin_f")):
                    dst = may_fill(pe, what)
                    did_fill(pe.matmul(dst, table(name), u_sb, start=True, stop=True), what)

            def to_time(b):
                pe.wait_ge(spec_ready, b + 1)
                dst = may_fill(pe, ("y", b))
                pe.matmul(dst, table("cos_t"), y_cos, start=True, stop=False)
                did_fill(pe.matmul(dst, table("sin_t"), y_sin, start=False, stop=True), ("y", b))

            def gate(b):
                pe.wait_ge(xn2_ready, b + 1)
                dst = may_fill(pe, ("x2T", b))
                for c in range(DCH):
                    ins = pe.transpose(dst[:, col_slice(c)], xn2[:, b, col_slice(c)], ident)
                did_fill(ins, ("x2T", b))
                dst = may_fill(pe, ("lg", b))
                pe.wait_ge(gate_loaded, 32)
                after_read(pe, ("x2T", b))
                for c in range(DCH):
                    ins = pe.matmul(dst[:, 0:NE], xn2_t[:, c, :], wg_sb[:, c, :], start=c == 0, stop=c == DCH - 1)
                did_fill(ins, ("lg", b))

            for j in range(NQ):
                turn_context(0, j)
                scores(0, j)
            for b in range(NB):
                for j in range(NQ):
                    turn_probs(b, j)
                    if b + 1 < NB:
                        turn_context(b + 1, j)
                        scores(b + 1, j)
                if b == 1:
                    kernel_products()
                if b >= 1:
                    values(b - 1)
                if b >= 2:
                    to_time(b - 2)
                probs_context(b)
                if b >= 1:
                    to_frequency(b - 1)
                if b >= 2:
                    gate(b - 2)
            values(3)
            to_time(2)
            to_frequency(3)
            gate(2)
            to_time(3)
            gate(3)

            dst = may_fill(pe, ("route",))
            pe.wait_ge(hot_ready, 1)
            for b in range(NB):
                for s in range(b + 1):
                    pe.matmul(dst[:, b * NE:(b + 1) * NE], ones if s < b else table("earlier"), hot[:, s, :],
                              start=s == 0, stop=s == b)
            for s in range(NB):
                ins = pe.matmul(dst[:, NB * NE:NB * NE + NE], ones, hot[:, s, :], start=s == 0, stop=s == NB - 1)
            did_fill(ins, ("route",))

            def gather(n):
                pe.wait_ge(onehot_ready, n)
                for c in range(DCH):
                    for b in range(NB):
                        ins = pe.matmul(bank[:, XW, c * SLOT:(c + 1) * SLOT], xn2[:, b, col_slice(c)],
                                        onehot_w[:, b, :], start=b == 0, stop=b == NB - 1)
                ins.then_inc(xw_filled, 1)

            def turn_outputs(w):
                for c in range(DCH):
                    ins = pe.transpose(bank[0:SLOT, YT, col_slice(c)], y_win[:, c, :], ident)
                ins.then_inc(yt_filled, 1)

            def outputs_may_turn(w):
                pe.wait_ge(y_ready, w + 1)
                pe.wait_ge(rows_out_ready, w + 1)

            def hidden(e, half, dst_bank, done, w=None):
                j = UNITS * e + half
                pe.wait_ge(place_loaded[weight_place(j)], 16 * weight_count(j))
                w1_half = ring[:, weight_place(j), :].rearrange("p (d m) -> p d m", d=DCH)
                for m in range(8):
                    if w is not None and m == 7:
                        outputs_may_turn(w)
                    for d in range(DCH):
                        ins = pe.matmul(bank[:, dst_bank, m * SLOT:(m + 1) * SLOT], w1_half[:, d, col_slice(m)],
                                        x_win[:, d, :], start=d == 0, stop=d == DCH - 1)
                ins.then_inc(done, 1)

            def output(e, half, done):
                j = UNITS * e + 2 + half
                pe.wait_ge(place_loaded[weight_place(j)], 16 * weight_count(j))
                w2_half = ring[:, weight_place(j), :].rearrange("p (m n) -> p m n", m=8)
                for m in range(8):
                    for c in range(DCH):
                        ins = pe.matmul(bank[:, YB, c * SLOT:(c + 1) * SLOT], w2_half[:, m, col_slice(c)],
                                        hid[:, 8 * half + m, :], start=half == 0 and m == 0 and c == 0,
                                        stop=half == 1 and m == 7, skip_group_check=True)
                ins.then_inc(done, 1)

            after_read(pe, ("qb",))
            gather(1)
            pe.wait_ge(windows_ready, 1)
            bounds = [pe.value_load(win_i[0:1, e:e + 1], min_val=0, max_val=MAXW) for e in range(NE + 1)]
            for e in range(NE):
                with pe.If(bounds[e] < bounds[e + 1]):
                    with pe.Fori(bounds[e], bounds[e + 1]) as w:
                        pe.wait_ge(xw_ready, w + 1)
                        hidden(e, 0, HA, ha_filled, w)
                        turn_outputs(w)
                        hidden(e, 1, HB, hb_filled)
                        gather(w + 2)
                        pe.wait_ge(ha_ready, w + 1)
                        output(e, 0, ya_done)
                        pe.wait_ge(hb_ready, w + 1)
                        output(e, 1, y_filled)
            outputs_may_turn(bounds[NE])
            pe.matmul(bank[:, YT, 0:1], ident, ones[:, 0:1], start=True, stop=True)
            turn_outputs(bounds[NE])


def shape_tables():
    import numpy as np

    t = np.zeros((P, TABLE_COLS), np.float32)

    def put(name, value):
        lo, hi = TABLES[name]
        t[:, lo:hi] = value

    p = np.arange(P)
    angle = np.pi * (((2 * p[None, :] + 1) * p[:, None]) % (4 * P)) / (2 * P)
    put("ident", np.eye(P))
    put("ones", 1.0)
    put("cos_f", np.cos(angle))
    put("sin_f", np.sin(angle))
    put("cos_t", np.cos(angle.T) / P)
    put("sin_t", np.sin(angle.T) / P)
    put("pick", np.arange(P + BL - 1)[None, :] == (BL * (p // HG) + BL - 1)[:, None])
    put("own", np.arange(HG)[None, :] == (p % HG)[:, None])
    put("earlier", p[:, None] < p[None, :])
    put("iota", np.arange(SLOT))
    put("rank_e", NE - np.arange(NE))
    put("before_e", (np.arange(NE)[None, :] < np.arange(NE + 1)[:, None]).ravel())
    put("steps", np.concatenate([BL * np.arange(AH), np.arange(BL)]))
    put("phase", np.where(p[:, None] < NS, [[0.25, 0.25, 0.5]], [[0.0, 0.5, 0.75]]))
    return t


def kernel(**inputs):
    import numpy as np
    import concourse.bacc as bacc
    from concourse.bass_utils import run_bass_kernel_spmd

    g = {k: np.asarray(v) for k, v in inputs.items()}
    nc = bacc.Bacc("TRN2", target_bir_lowering=False, num_devices=1)
    w_re_t, w_im_t = g["L0_attn_W_re"].T, g["L0_attn_W_im"].T
    lam = np.stack([g["L0_attn_Lambda_re"], g["L0_attn_Lambda_im"]], 1)
    arrays = {
        "x": g["x"].reshape(NB * LQ, D),
        "ctx": g["ctx_512"],
        "wq_t": g["L0_xattn_Wq"].T,
        "wk_t": g["L0_xattn_Wk"].T,
        "bkq": np.stack([g["L0_xattn_bk"], g["L0_xattn_bq"]], 1),
        "wv": g["L0_xattn_Wv"],
        "bv": g["L0_xattn_bv"],
        "log_dt": g["L0_attn_log_dt"],
        "w_ri": np.stack([np.concatenate([w_re_t, w_re_t]), np.concatenate([w_im_t, w_im_t])]),
        "lam": np.concatenate([lam, lam]),
        "d_skip": g["L0_attn_D"].reshape(1, D),
        "w_gate": g["L0_ffn_w_gate"],
        "b_gate": g["L0_ffn_b_gate"],
        "w1": g["L0_ffn_W1"],
        "b1": g["L0_ffn_b1"].reshape(NE, MCH, P).transpose(2, 0, 1),
        "w2": g["L0_ffn_W2"],
        "b2": g["L0_ffn_b2"].reshape(NE, DCH, P).transpose(2, 0, 1),
        "tables": shape_tables(),
    }
    arrays = {f"in_{k}": np.ascontiguousarray(v) for k, v in arrays.items()}
    args = [nc.dram_tensor(k, v.shape, mybir.dt.from_np(v.dtype), kind="ExternalInput").ap()
            for k, v in arrays.items()]
    out = nc.dram_tensor("out", (NB * LQ, D), F32, kind="ExternalOutput").ap()
    perceiver_layer(nc, *args, out)
    r = run_bass_kernel_spmd(nc, [arrays], core_ids=[0])
    return r.results[0]["out"].reshape(NB, LQ, D)
```

```python
from contextlib import ExitStack

import concourse.bass as bass
from concourse import mybir

F32 = mybir.dt.float32
I32 = mybir.dt.int32
U32 = mybir.dt.uint32
ALU = mybir.AluOpType
ACT = mybir.ActivationFunctionType
AX = mybir.AxisListType.X

P = 128
NB, LQ, D = 4, 128, 512
LK, DC = 2048, 256
NS = 64
NE, DM = 8, 2048
DCH, CCH, MCH = D // P, DC // P, DM // P
KCH = LK // P
NQ = 4
KPQ = KCH // NQ
AH, BL = 16, 8
HG = P // AH
MAXW = NE + (NB * LQ - NE) // P
HB_CH = 4
NB2 = 4
NSLOT = 10
UNITS = 4
EPS = 1e-5
ROUND = 1.5 * 2.0 ** 23
TWO_PI = 6.283185307179586

TABLES = {}
_at = 0
for _name, _n in (("ident", P), ("ones", P), ("cos_f", P), ("sin_f", P), ("cos_t", P), ("sin_t", P),
                  ("pick", P + BL - 1), ("own", HG), ("earlier", P), ("iota", P), ("blocks", NB), ("rank_e", NE),
                  ("before_e", (NE + 1) * NE), ("steps", AH + BL), ("phase", 3)):
    TABLES[_name] = (_at, _at + _n)
    _at += _n
TABLE_COLS = _at
COLS = 144

S_BANK = [0, 1, 2, 3]
T0, T1, T2, O_BANK = 4, 5, 6, 7
H_BANK, T_BANK, Y_BANK = (4, 5), (6, 7), 0

FILLS = [(S_BANK[d], ("wqk", d)) for d in range(DCH)] + [(O_BANK, ("bias",))]
FILLS += [((T0, T1, T2, T0)[b], ("xnT", b)) for b in range(NB)]
FILLS += [(S_BANK[c], ("q", c)) for c in range(CCH)] + [(O_BANK, ("qb",))]


def _context_fills(b, j):
    return [(T0, ("ct", b, j, 0)), (T1, ("ct", b, j, 1)), (S_BANK[j], ("s", b, j))]


def _kernel_fills():
    out = [((T0, T1)[g % 2], ("k1", g)) for g in range(8)]
    return out + [(T2, ("k2",)), (T0, ("k3", 0)), (T1, ("k3", 1))]


def _value_fills(b):
    return [(T2, ("anT", b)), (T0, ("av", b))]


def _freq_fills(b):
    return [(T1, ("uc", b)), (T2, ("us", b))]


def _time_fills(b):
    return [(T0, ("y", b))]


def _gate_fills(b):
    return [(T1, ("x2T", b)), (T2, ("lg", b))]


for _j in range(NQ):
    FILLS += _context_fills(0, _j)
for _b in range(NB):
    for _j in range(NQ):
        FILLS.append((T2, ("pT", _b, _j)))
        if _b + 1 < NB:
            FILLS += _context_fills(_b + 1, _j)
    if _b == 1:
        FILLS += _kernel_fills()
    if _b >= 1:
        FILLS += _value_fills(_b - 1)
    if _b >= 2:
        FILLS += _time_fills(_b - 2)
    FILLS.append((O_BANK, ("pv", _b)))
    if _b >= 1:
        FILLS += _freq_fills(_b - 1)
    if _b >= 2:
        FILLS += _gate_fills(_b - 2)
FILLS += (_value_fills(3) + _time_fills(2) + _freq_fills(3) + _gate_fills(2) + _time_fills(3)
          + _gate_fills(3) + [(T0, ("route",))] + [(S_BANK[c], ("xs", c)) for c in range(DCH)])

FILL_NO = {}
FILL_COUNT = [0] * 8
for _bank, _what in FILLS:
    FILL_COUNT[_bank] += 1
    FILL_NO[_what] = (_bank, FILL_COUNT[_bank])


def perceiver_layer(nc, x, ctx, wq_t, wk_t, bkq, wv, bv, log_dt, w_ri, lam, d_skip,
                    w_gate, b_gate, w1, b1, w2, b2, tables, out):
    x_rows = x.rearrange("(b t) h -> t b h", t=P)
    out_rows = out.rearrange("(b t) h -> t b h", t=P)
    y_rows = nc.dram_tensor("y_rows", ((NB + 1) * P, D), F32, kind="Internal").ap()

    with ExitStack() as stack:
        def sb(name, shape, dt=F32):
            return stack.enter_context(nc.sbuf_tensor(name, shape, dt))

        def sem(name):
            return stack.enter_context(nc.semaphore(name))

        bank = stack.enter_context(nc.psum_tensor("bank", [P, 8, 512], F32))

        ring = sb("ring", [P, NSLOT, 4096])
        x_sb = sb("x_sb", [P, NB, D])
        work = sb("work", [P, 4096])
        hbuf = sb("hbuf", [P, 1024])
        late = sb("late", [P, 5 * D])
        kfreq = late[:, 0:2 * D].rearrange("p (k h) -> p k h", k=2)
        wri = late[:, 2 * D:4 * D].rearrange("p (k h) -> p k h", k=2)
        dt_sb = late[:, 4 * D:5 * D]
        xs_t = late[:].rearrange("p (c n) -> p c n", c=DCH)
        small = sb("small", [P, 1024])
        tab = sb("tab", [P, TABLE_COLS])
        cols = sb("cols", [P, COLS])
        icols = sb("icols", [P, 24], I32)

        def table(name):
            lo, hi = TABLES[name]
            return tab[:, lo:hi]

        ident, ones = table("ident"), table("ones")

        ctx_sb = [ring[:, b, :].rearrange("p (k c) -> p k c", k=KCH) for b in range(NB)]
        a_sin = ring[:, 2:4, :].rearrange("p s (a h) -> p (s a) h", h=D)
        a_tab = ring[:, 6:8, :].rearrange("p s (a h) -> p (s a) h", h=D)
        b_tab = ring[:, 4, :].rearrange("p (b h) -> p b h", h=D)
        b_sin1 = ring[:, 5, :].rearrange("p (b h) -> p b h", h=D)
        k_parts = ring[:, 5, :].rearrange("p (b h) -> p b h", h=D)
        b_sin2 = work[:].rearrange("p (b h) -> p b h", h=D)
        xn2 = work[:, 0:2048].rearrange("p (b h) -> p b h", h=D)
        y_cos, y_sin, prod1, prod2 = (work[:, 2048 + i * D:2560 + i * D] for i in range(4))
        scratch = ring[:, 8:10, :].rearrange("p s n -> p (s n)")
        xn1 = scratch[:, 0:2048].rearrange("p (b h) -> p b h", h=D)
        probs = scratch[:, 0:2048]
        xn1_t = scratch[:, 2048:4096].rearrange("p (c n) -> p c n", c=DCH)
        probs_t = scratch[:, 2048:4096].rearrange("p (k n) -> p k n", k=KCH)
        wq_sb = scratch[:, 4096:6144].rearrange("p (e d) -> p e d", e=DCH)
        ctx_t = scratch[:, 4096:6144].rearrange("p (u c n) -> p u c n", u=2, c=CCH)
        wk_sb = scratch[:, 6144:7168].rearrange("p (e c) -> p e c", e=DCH)
        q_t = scratch[:, 6144:7168].rearrange("p (c n) -> p c n", c=CCH)
        wqk = scratch[:, 7168:8192].rearrange("p (d c) -> p d c", d=DCH)
        bv_sb = kfreq[:, 0, :]
        u_sb = wri[:, 0, :]
        xn2_t = wri[:, 1, :].rearrange("p (c n) -> p c n", c=DCH)
        an = dt_sb[:, 0:DC]
        an_t = dt_sb[:, DC:2 * DC].rearrange("p (c n) -> p c n", c=CCH)
        round_v = hbuf[:].rearrange("p (a h) -> p a h", h=D)
        wv_sb = hbuf[:].rearrange("p (c n) -> p c n", c=CCH)
        hid_t = hbuf[:].rearrange("p (y m s) -> p y m s", y=2, m=HB_CH)
        round_g = small[:].rearrange("p (a h) -> p a h", h=D)
        k_time = small[:, 0:D]
        b1_sb = small[:, 0:NE * MCH].rearrange("p (e c) -> p e c", e=NE)
        y_out = small[:, 512:1024]
        onehot = work[:, 2048:4096].rearrange("p (b s) -> p b s", b=NB)
        b2_sb = [work[:, i * D:(i + 1) * D] for i in range(NB2)]
        hid, x_win_2d, y_raw = [work[:, 2048 + i * D:2560 + i * D] for i in range(2)], work[:, 3072:3584], work[:, 3584:4096]
        x_win = x_win_2d.rearrange("p (c n) -> p c n", c=DCH)
        y_tok = xn2

        _next = [0]

        def col(n):
            _next[0] += n
            assert _next[0] <= COLS
            return cols[:, _next[0] - n:_next[0]]

        lam_c, decay = col(2), col(1)
        step_mag, step_ph = col(AH + BL), col(AH + BL)
        bn6, mv = col(6), col(2 * NB)
        rstd, var_eps, m_half = col(NB), col(NB), col(NB)
        bkq_sb = col(2 * DCH).rearrange("p (e k) -> p e k", k=2)
        bkq_prod, bkq_sum = col(DCH), col(1)
        qbias, wqb, q_bk = col(3), col(DCH), col(NB)
        qmax, rsum, nbias = col(NB * NQ), col(NB * NQ), col(NB)
        rmax, rmax_q, rtot = col(1), col(1), col(1)
        spare = qmax
        logits = tab[:, TABLES["pick"][0]:TABLES["pick"][0] + NB * NE].rearrange("p (b e) -> p b e", e=NE)
        rt0 = TABLES["cos_f"][0]

        def route(i, n):
            return tab[:, rt0 + i:rt0 + i + n]

        lmax = route(0, 4)
        lsub = route(4, 32).rearrange("p (b e) -> p b e", e=NE)
        first = route(36, 32).rearrange("p (b e) -> p b e", e=NE)
        hot = route(68, 32).rearrange("p (b e) -> p b e", e=NE)
        fmax = route(100, 4)
        psum_e, prob = route(104, 4), route(108, 4)
        rt1 = TABLES["sin_f"][0]
        lexp = tab[:, rt1:rt1 + 32].rearrange("p (b e) -> p b e", e=NE)
        nwin = tab[:, rt1 + 32:rt1 + 40]
        cum9 = tab[:, rt1 + 40:rt1 + 49]
        slot_e = tab[:, rt1 + 57:rt1 + 89].rearrange("p (b e) -> p b e", e=NE)
        slot = tab[:, rt1 + 89:rt1 + 93]
        rt2 = TABLES["cos_t"][0]
        cum_prod = tab[:, rt2:rt2 + 72].rearrange("p (e f) -> p e f", f=NE)
        slot_k = tab[:, rt2 + 72:rt2 + 88].rearrange("p (b k) -> p b k", b=NB)
        off9 = tab[:, rt2 + 88:rt2 + 97]
        win_i = icols[:, 0:NE + 1]
        off_i = icols[:, 9:17]
        row_i = icols[:, 17:21].bitcast(U32)
        wg_sb = sb("wg_sb", [P, DCH, NE])
        bg_sb = sb("bg_sb", [P, NE])
        d_sb = kfreq[0:1, 1, :]

        filled = [sem(f"bank{k}_filled") for k in range(8)]
        drained = [sem(f"bank{k}_drained") for k in range(8)]
        place_loaded = [sem(f"place{k}_loaded") for k in range(NSLOT)]
        params_loaded, tab_loaded, x_loaded = sem("params_loaded"), sem("tab_loaded"), sem("x_loaded")
        qk_loaded, bv_loaded, wri_loaded = sem("qk_loaded"), sem("bv_loaded"), sem("wri_loaded")
        wv_loaded, gate_loaded, d_loaded = sem("wv_loaded"), sem("gate_loaded"), sem("d_loaded")
        bias_loaded = sem("bias_loaded")
        b2_loaded = [sem(f"b2_{i}_loaded") for i in range(NB2)]
        dve_step = sem("dve_step")
        pool_step = sem("pool_step")
        dt_ready, step_mag_ready, step_ph_ready = sem("dt_ready"), sem("step_mag_ready"), sem("step_ph_ready")
        half_ready, zeros_ready, mags_ready = sem("half_ready"), sem("zeros_ready"), sem("mags_ready")
        a_phase_ready, b_phase_ready = sem("a_phase_ready"), sem("b_phase_ready")
        a_sin_ready, b_sin_ready, wr_done = sem("a_sin_ready"), sem("b_sin_ready"), sem("wr_done")
        a_tab_ready, b_tab_ready = sem("a_tab_ready"), sem("b_tab_ready")
        var_ready, rstd_ready = sem("var_ready"), sem("rstd_ready")
        xn1_ready, bkq_ready, rmax_ready = sem("xn1_ready"), sem("bkq_ready"), sem("rmax_ready")
        u_ready, spec_ready, xn2_ready = sem("u_ready"), sem("spec_ready"), sem("xn2_ready")
        hot_ready, lsub_ready, lexp_ready = sem("hot_ready"), sem("lsub_ready"), sem("lexp_ready")
        windows_ready, rows_ready = sem("windows_ready"), sem("rows_ready")
        onehot_ready, pad_ready, xw_ready = sem("onehot_ready"), sem("pad_ready"), sem("xw_ready")
        h_filled = [sem(f"h{p}_filled") for p in range(2)]
        h_copied = [sem(f"h{p}_copied") for p in range(2)]
        t_filled = [sem(f"t{p}_filled") for p in range(2)]
        h_ready = [sem(f"h{p}_ready") for p in range(2)]
        o_done = [sem(f"o{p}_done") for p in range(2)]
        y_copied, y_added, rows_sent = sem("y_copied"), sem("y_added"), sem("rows_sent")
        gathered = [sem(f"gathered{b}") for b in range(NB)]
        result_ready, result_sent = sem("result_ready"), sem("result_sent")

        def weight_place(j):
            return (4, 5, 6, 7, 0, 1, 2, 3, 8, 9)[j % NSLOT]

        def weight_count(j):
            return j // NSLOT + (2 if weight_place(j) < NB else 1)

        def after_fill(eng, what):
            b, n = FILL_NO[what]
            eng.wait_ge(filled[b], n)

        def after_read(eng, what):
            b, n = FILL_NO[what]
            eng.wait_ge(drained[b], n)

        def may_fill(eng, what):
            b, n = FILL_NO[what]
            if n > 1:
                eng.wait_ge(drained[b], n - 1)
            return bank[:, b, :]

        def did_fill(ins, what):
            ins.then_inc(filled[FILL_NO[what][0]], 1)

        def may_read(eng, what):
            after_fill(eng, what)
            return bank[:, FILL_NO[what][0], :]

        def did_read(ins, what):
            ins.then_inc(drained[FILL_NO[what][0]], 1)

        def sorted_tokens(eng, c, copy):
            src = may_read(eng, ("xs", c))
            did_read(copy(xs_t[:, c, 0:NB * P], src), ("xs", c))

        def window_row(offset, i):
            return nc.s_assert_within(offset + i * P, 0, NB * P,
                                      skip_runtime_bounds_check_because="windows cover only the tokens there are")

        def hidden_may_copy(eng, parity, w, k):
            eng.wait_ge(h_filled[parity], 2 * w + k + 3)
            eng.wait_ge(t_filled[parity], 2 * w + k + 1)

        block = stack.enter_context(nc.Block())

        @block.sync
        def _(sp):
            sp.dma_start(x_sb[:], x_rows).then_inc(x_loaded, 16)
            sp.dma_start(wk_sb, wk_t.rearrange("(e p) c -> p e c", p=P)).then_inc(qk_loaded, 16)
            sp.dma_start(wq_sb, wq_t.rearrange("(e p) d -> p e d", p=P)).then_inc(qk_loaded, 16)
            for b in range(NB):
                if b == 2:
                    sp.wait_ge(a_tab_ready, 1)
                sp.dma_start(ring[:, b, :], ctx[b].rearrange("(p k) c -> p (k c)", p=P)) \
                    .then_inc(place_loaded[b], 16)
            sp.dma_start(wv_sb, wv.rearrange("(c p) n -> p c n", p=P)).then_inc(wv_loaded, 16)

            def load_unit(j):
                e, u = divmod(j, UNITS)
                place = ring[:, weight_place(j), :]
                if u < 2:
                    src = w1[e].rearrange("(d p) m -> p d m", p=P)[:, :, u * 1024:(u + 1) * 1024]
                    dst = place.rearrange("p (d m) -> p d m", d=DCH)
                else:
                    src = w2[e].rearrange("(m p) n -> p m n", p=P)[:, (u - 2) * 8:(u - 1) * 8, :]
                    dst = place.rearrange("p (m n) -> p m n", m=8)
                sp.dma_start(dst, src).then_inc(place_loaded[weight_place(j)], 16)

            for j in range(NSLOT):
                if j == 0:
                    after_fill(sp, ("k1", 7))
                if j == 1:
                    after_fill(sp, ("k2",))
                if 4 <= j < 8:
                    after_fill(sp, ("pv", j - 4))
                load_unit(j)
            sp.wait_ge(windows_ready, 1)
            last = [sp.value_load(win_i[0:1, e + 1:e + 2], min_val=0, max_val=MAXW) for e in range(NE)]

            def load_b2(e):
                sp.dma_start(b2_sb[e % NB2], b2[e].partition_broadcast(P)).then_inc(b2_loaded[e % NB2], 16)

            after_fill(sp, ("xs", DCH - 1))
            for e in range(NB2):
                load_b2(e)
            for j in range(NSLOT, NE * UNITS):
                e, u = divmod(j - NSLOT, UNITS)
                if u == 0 and 1 <= e <= NE - NB2:
                    sp.wait_ge(y_added, last[e - 1] + 1)
                    sp.wait_ge(b2_loaded[e - 1], 16)
                    load_b2(e - 1 + NB2)
                sp.wait_ge((h_filled if u < 2 else o_done)[1], 2 * last[e] + 1 + u % 2)
                sp.wait_ge(place_loaded[weight_place(j)], 16 * (weight_count(j) - 1))
                load_unit(j)
            for b in range(NB):
                sp.wait_ge(result_ready, b + 1)
                sp.dma_start(out_rows[:, b, :], x_sb[:, b, :]).then_inc(result_sent, 16)
            sp.wait_ge(result_sent, 16 * NB)
            sp.dma_start(cols[:, 0:2], lam).then_inc(params_loaded, 16)
            sp.wait_ge(params_loaded, 48)

        @block.scalar
        def _(act):
            act.dma_start(lam_c, lam).then_inc(params_loaded, 16)
            act.dma_start(dt_sb, log_dt.partition_broadcast(P)).then_inc(params_loaded, 16)
            act.dma_start(tab[:], tables).then_inc(tab_loaded, 16)
            act.dma_start(bv_sb, bv.partition_broadcast(P)).then_inc(bv_loaded, 16)
            act.dma_start(bkq_sb, bkq.rearrange("(e p) k -> p e k", p=P)).then_inc(qk_loaded, 16)
            act.dma_start(wri, w_ri.rearrange("k n h -> n k h")).then_inc(wri_loaded, 16)
            act.dma_start(wg_sb[:], w_gate.rearrange("(c p) e -> p c e", p=P)).then_inc(gate_loaded, 16)
            act.dma_start(bg_sb[:], b_gate.partition_broadcast(P)).then_inc(gate_loaded, 16)
            act.dma_start(d_sb, d_skip).then_inc(d_loaded, 16)

            act.wait_ge(params_loaded, 32)
            act.activation(decay, lam_c[:, 0:1], ACT.Exp).then_inc(dt_ready, 1)
            act.activation(dt_sb, dt_sb, ACT.Exp).then_inc(dt_ready, 1)

            act.wait_ge(dt_ready, 2)
            act.wait_ge(step_mag_ready, 1)
            for i in range(AH + BL):
                dst = a_tab[:, i, :] if i < AH else b_tab[:, i - AH, :]
                ins = act.activation(dst, dt_sb, ACT.Exp, scale=step_mag[:, i:i + 1])
            ins.then_inc(mags_ready, 1)

            after_read(act, ("bias",))
            for c in range(CCH):
                src = may_read(act, ("q", c))
                did_read(act.activation(q_t[:, c, :], src, ACT.Identity, bias=qbias[:, c:c + 1]), ("q", c))

            for i in range(4):
                act.wait_ge(a_phase_ready, 2 * i + 2)
                sines = a_sin[:, 4 * i:4 * i + 4, :]
                act.activation(sines, sines, ACT.Sin, scale=-TWO_PI).then_inc(a_sin_ready, 1)
            for i in range(4):
                act.wait_ge(b_phase_ready, 2 * i + 2)
                sines = (b_sin1, b_sin2)[i // 2][:, 4 * (i % 2):4 * (i % 2) + 4, :]
                act.activation(sines, sines, ACT.Sin, scale=-TWO_PI).then_inc(b_sin_ready, 1)

            def softmax_exp(b):
                act.wait_ge(rmax_ready, b + 1)
                for j in range(NQ):
                    if b > 0:
                        after_fill(act, ("pT", b - 1, j))
                    src = may_read(act, ("s", b, j))
                    did_read(act.activation(probs[:, j * 512:(j + 1) * 512], src, ACT.Exp,
                                            bias=nbias[:, b:b + 1], accum_out=rsum[:, NQ * b + j:NQ * b + j + 1]),
                             ("s", b, j))

            def turned_gate_rows(b):
                src = may_read(act, ("x2T", b))
                if b > 0:
                    after_fill(act, ("lg", b - 1))
                did_read(act.activation(xn2_t, src.rearrange("p (c n) -> p c n", c=DCH), ACT.Identity), ("x2T", b))

            softmax_exp(0)
            for b in range(NB):
                for j in range(NQ):
                    if j % 2:
                        src = may_read(act, ("pT", b, j))
                        if b > 0:
                            after_fill(act, ("pv", b - 1))
                        did_read(act.activation(probs_t[:, KPQ * j:KPQ * j + KPQ, :],
                                                src.rearrange("p (k n) -> p k n", k=KPQ), ACT.Identity),
                                 ("pT", b, j))
                    if b + 1 < NB:
                        src = may_read(act, ("ct", b + 1, j, 1))
                        after_fill(act, ("s", b + 1, j - 2) if j >= 2 else ("s", b, j + 2))
                        did_read(act.activation(ctx_t[:, j % 2, 1, :], src, ACT.Identity), ("ct", b + 1, j, 1))
                if b + 1 < NB:
                    softmax_exp(b + 1)
                if b >= 2:
                    turned_gate_rows(b - 2)
            turned_gate_rows(2)
            turned_gate_rows(3)
            after_fill(act, ("k3", 1))
            act.dma_start(b1_sb, b1).then_inc(bias_loaded, 16)
            act.wait_ge(lsub_ready, 1)
            act.activation(lexp, lsub, ACT.Exp).then_inc(lexp_ready, 1)
            for c in range(0, DCH, 2):
                sorted_tokens(act, c, lambda dst, src: act.activation(dst, src, ACT.Identity))

            act.wait_ge(bias_loaded, 16)
            act.wait_ge(windows_ready, 2)
            bounds = [act.value_load(win_i[0:1, e:e + 1], min_val=0, max_val=MAXW) for e in range(NE + 1)]
            for e in range(NE):
                with act.If(bounds[e] < bounds[e + 1]):
                    with act.Fori(bounds[e], bounds[e + 1]) as w:
                        for k in range(2):
                            hidden_may_copy(act, 0, w, k)
                            act.activation(hid[0], bank[:, H_BANK[0], :], ACT.Identity).then_inc(h_copied[0], 1)
                            act.wait_ge(t_filled[0], 2 * w + k + 2)
                            act.wait_ge(o_done[0], 2 * w + k + 2)
                            for i in range(HB_CH):
                                m = 2 * HB_CH * k + i
                                ins = act.activation(hid_t[:, 0, i, :], bank[:, T_BANK[0], i * P:(i + 1) * P], ACT.Relu,
                                                     bias=b1_sb[:, e, m:m + 1])
                            ins.then_inc(h_ready[0], 1)
                        act.wait_ge(o_done[1], 2 * w + 4)
                        act.wait_ge(y_added, w + 1)
                        act.activation(y_raw, bank[:, Y_BANK, :], ACT.Identity).then_inc(y_copied, 1)

        @block.vector
        def _(dve):
            steps = [0]

            def link(ins):
                steps[0] += 1
                ins.then_inc(dve_step, 1)
                dve.wait_ge(dve_step, steps[0])

            dve.memset(m_half, -0.5).then_inc(half_ready, 1)
            dve.wait_ge(tab_loaded, 16)
            dve.wait_ge(dt_ready, 2)
            dve.tensor_scalar(step_mag, table("steps"), decay, -1.0, ALU.mult, ALU.mult).then_inc(step_mag_ready, 1)
            dve.tensor_scalar(step_ph, table("steps"), lam_c[:, 1:2], 1.0 / TWO_PI, ALU.mult, ALU.mult) \
                .then_inc(step_ph_ready, 1)

            norms = [0]

            def layer_norm(tiles, dst):
                n = len(tiles)
                for i, t in enumerate(tiles):
                    link(dve.bn_stats(bn6, x_sb[:, t, :]))
                    link(dve.bn_aggr(mv[:, 2 * i:2 * i + 2], bn6))
                var = mv.rearrange("p (t k) -> p t k", k=2)[:, 0:n, 1:2]
                dve.tensor_scalar(var_eps[:, 0:n].unsqueeze(2), var, EPS, None, ALU.add).then_inc(var_ready, 1)
                norms[0] += 1
                dve.wait_ge(rstd_ready, norms[0])
                for i, t in enumerate(tiles):
                    ins = dve.tensor_scalar(dst[i], x_sb[:, t, :], mv[:, 2 * i:2 * i + 1], rstd[:, i:i + 1],
                                            ALU.subtract, ALU.mult)
                return ins

            dve.wait_ge(x_loaded, 16)
            layer_norm(range(NB), [xn1[:, b, :] for b in range(NB)]).then_inc(xn1_ready, 1)

            dve.wait_ge(qk_loaded, 48)
            link(dve.tensor_tensor(bkq_prod, bkq_sb[:, :, 0], bkq_sb[:, :, 1], ALU.mult))
            dve.tensor_reduce(bkq_sum, bkq_prod, AX, ALU.add).then_inc(bkq_ready, 1)
            for d in range(DCH):
                src = may_read(dve, ("wqk", d))
                dve.tensor_copy(wqk[:, d, :], src[:, 0:DC])
                did_read(dve.tensor_copy(wqb[:, d:d + 1], src[:, DC:DC + 1]), ("wqk", d))
            src = may_read(dve, ("bias",))
            did_read(dve.tensor_copy(qbias, src[:, 0:3]), ("bias",))
            for b in range(NB):
                src = may_read(dve, ("xnT", b))
                did_read(dve.tensor_copy(xn1_t[:, :, b * P:(b + 1) * P], src.rearrange("p (c n) -> p c n", c=DCH)),
                         ("xnT", b))
            dve.wait_ge(xn1_ready, 1)
            dve.wait_ge(bv_loaded, 16)
            link(dve.tensor_tensor(x_sb[:], x_sb[:], bv_sb.unsqueeze(1).to_broadcast([P, NB, D]), ALU.add))
            src = may_read(dve, ("qb",))
            after_read(dve, ("bias",))
            did_read(dve.tensor_scalar(q_bk, src[:, 0:NB], qbias[:, 2:3], None, ALU.add), ("qb",))

            dve.wait_ge(step_ph_ready, 1)
            for i in range(AH // 2):
                turns = a_sin[:, 2 * i:2 * i + 2, :]
                for a in (2 * i, 2 * i + 1):
                    ins = dve.tensor_scalar(a_sin[:, a, :], dt_sb, step_ph[:, a:a + 1], table("phase")[:, 0:1],
                                            ALU.mult, ALU.add)
                link(ins)
                link(dve.tensor_scalar(round_v, turns, ROUND, None, ALU.add))
                dve.scalar_tensor_tensor(out=turns, in0=round_v, scalar=ROUND, in1=turns, op0=ALU.subtract,
                                         op1=ALU.subtract).then_inc(a_phase_ready, 1)

            def context_read(b, j):
                for c in range(CCH if b == 0 else 1):
                    src = may_read(dve, ("ct", b, j, c))
                    if j >= 2:
                        after_fill(dve, ("s", b, j - 2))
                    elif b > 0:
                        after_fill(dve, ("s", b - 1, j + 2))
                    did_read(dve.tensor_copy(ctx_t[:, j % 2, c, :], src), ("ct", b, j, c))

            def quarter_max(b, j):
                src = may_read(dve, ("s", b, j))
                return dve.tensor_reduce(qmax[:, NQ * b + j:NQ * b + j + 1], src, AX, ALU.max)

            def row_bias(b):
                link(dve.tensor_reduce(rmax, qmax[:, NQ * b:NQ * b + NQ], AX, ALU.max))
                link(dve.tensor_tensor(rmax_q, rmax, q_bk[:, b:b + 1], ALU.add))
                dve.tensor_tensor(nbias[:, b:b + 1], q_bk[:, b:b + 1], rmax_q, ALU.subtract).then_inc(rmax_ready, 1)

            for j in range(NQ):
                context_read(0, j)
                if j > 0:
                    quarter_max(0, j - 1)
            link(quarter_max(0, NQ - 1))
            row_bias(0)
            dve.wait_ge(mags_ready, 1)
            for i in range(4):
                dve.wait_ge(a_sin_ready, i + 1)
                rows = slice(4 * i, 4 * i + 4)
                ins = dve.tensor_tensor(a_tab[:, rows, :], a_tab[:, rows, :], a_sin[:, rows, :], ALU.mult)
            ins.then_inc(a_tab_ready, 1)

            def b_table():
                dve.wait_ge(b_sin_ready, 4)
                dve.wait_ge(wri_loaded, 16)
                link(dve.tensor_tensor(b_sin2, b_sin2, wri[:, 1, :].unsqueeze(1).to_broadcast([P, BL, D]), ALU.mult))
                dve.wait_ge(wr_done, 1)
                link(dve.tensor_tensor(b_sin1, b_sin1, b_sin2, ALU.add))
                dve.tensor_tensor(b_tab, b_tab, b_sin1, ALU.mult).then_inc(b_tab_ready, 1)

            def kernel_reads():
                own = table("own").unsqueeze(1).unsqueeze(1).to_broadcast([P, 8, BL, HG])
                for g in range(8):
                    src = may_read(dve, ("k1", g)).rearrange("p (g b h) -> p g b h", g=8, b=BL)
                    if g == 0:
                        dve.wait_ge(b_tab_ready, 1)
                    dst = k_parts.rearrange("p b (h g) -> p g b h", h=HG)[:, 8 * g:8 * g + 8, :, :]
                    did_read(dve.tensor_tensor(dst, src, own, ALU.mult), ("k1", g))
                src = may_read(dve, ("k2",))
                dve.wait_ge(b_phase_ready, 8)
                link(dve.tensor_copy(k_time, src))
                dve.wait_ge(d_loaded, 16)
                did_read(dve.tensor_tensor(k_time[0:1, :], k_time[0:1, :], d_sb, ALU.add), ("k2",))
                for i in range(2):
                    src = may_read(dve, ("k3", i))
                    did_read(dve.tensor_copy(kfreq[:, i, :], src), ("k3", i))

            def attention_out(b):
                src = may_read(dve, ("pv", b))
                link(dve.tensor_reduce(rtot, rsum[:, NQ * b:NQ * b + NQ], AX, ALU.add))
                link(dve.reciprocal(rtot, rtot))
                if b == 0:
                    dve.wait_ge(b_phase_ready, 8)
                did_read(dve.tensor_scalar(an, src[:, 0:DC], rtot, None, ALU.mult), ("pv", b))

            def value_reads(b):
                src = may_read(dve, ("anT", b))
                did_read(dve.tensor_copy(an_t, src[:, 0:DC].rearrange("p (c n) -> p c n", c=CCH)), ("anT", b))
                src = may_read(dve, ("av", b))
                did_read(dve.tensor_tensor(x_sb[:, b, :], src, x_sb[:, b, :], ALU.add), ("av", b))
                after_read(dve, ("av", b))
                if b == 0:
                    dve.wait_ge(wr_done, 1)
                layer_norm([b], [u_sb]).then_inc(u_ready, 1)

            def freq_reads(b):
                uc, us = may_read(dve, ("uc", b)), may_read(dve, ("us", b))
                kc, ks = kfreq[:, 0, :], kfreq[:, 1, :]
                dve.tensor_tensor(prod1, uc, ks, ALU.mult)
                did_read(dve.tensor_tensor(y_cos, uc, kc, ALU.mult), ("uc", b))
                dve.tensor_tensor(prod2, us, ks, ALU.mult)
                did_read(dve.tensor_tensor(y_sin, us, kc, ALU.mult), ("us", b))
                after_read(dve, ("us", b))
                dve.tensor_tensor(y_cos, y_cos, prod2, ALU.subtract)
                dve.tensor_tensor(y_sin, y_sin, prod1, ALU.add).then_inc(spec_ready, 1)

            def time_reads(b):
                src = may_read(dve, ("y", b))
                did_read(dve.tensor_tensor(x_sb[:, b, :], src, x_sb[:, b, :], ALU.add), ("y", b))
                after_read(dve, ("y", b))
                layer_norm([b], [xn2[:, b, :]]).then_inc(xn2_ready, 1)

            def gate_reads(b):
                dve.wait_ge(gate_loaded, 32)
                src = may_read(dve, ("lg", b))
                did_read(dve.tensor_tensor(logits[:, b, :], src[:, 0:NE], bg_sb[:], ALU.add), ("lg", b))

            for b in range(NB):
                for j in range(NQ):
                    if j % 2 == 0:
                        src = may_read(dve, ("pT", b, j))
                        if b > 0:
                            after_fill(dve, ("pv", b - 1))
                        did_read(dve.tensor_copy(probs_t[:, KPQ * j:KPQ * j + KPQ, :],
                                                 src.rearrange("p (k n) -> p k n", k=KPQ)), ("pT", b, j))
                    if b + 1 < NB:
                        context_read(b + 1, j)
                        ins = quarter_max(b + 1, j)
                if b + 1 < NB:
                    link(ins)
                    row_bias(b + 1)
                if b == 0:
                    b_table()
                if b == 1:
                    kernel_reads()
                if b >= 1:
                    value_reads(b - 1)
                if b >= 2:
                    time_reads(b - 2)
                attention_out(b)
                if b >= 1:
                    freq_reads(b - 1)
                if b >= 2:
                    gate_reads(b - 2)
            value_reads(3)
            time_reads(2)
            freq_reads(3)
            gate_reads(2)
            time_reads(3)
            gate_reads(3)

            def per_e(v):
                return v.unsqueeze(2).to_broadcast([P, NB, NE])

            after_read(dve, ("lg", 3))
            link(dve.tensor_reduce(lmax, logits, AX, ALU.max))
            link(dve.tensor_tensor(first, logits, per_e(lmax), ALU.is_equal))
            link(dve.tensor_tensor(first, first, table("rank_e").unsqueeze(1).to_broadcast([P, NB, NE]), ALU.mult))
            link(dve.tensor_reduce(fmax, first, AX, ALU.max))
            dve.tensor_tensor(hot, first, per_e(fmax), ALU.is_equal).then_inc(hot_ready, 1)
            dve.tensor_tensor(lsub, logits, per_e(lmax), ALU.subtract).then_inc(lsub_ready, 1)

            src = may_read(dve, ("route",))
            ranks = src[:, 0:NB * NE].rearrange("p (b e) -> p b e", e=NE)
            counts = src[:, NB * NE:NB * NE + NE]
            before = table("before_e").rearrange("p (e f) -> p e f", f=NE)
            link(dve.tensor_tensor(cum_prod, before, counts.unsqueeze(1).to_broadcast([P, NE + 1, NE]), ALU.mult))
            link(dve.tensor_reduce(off9, cum_prod, AX, ALU.add))
            dve.tensor_scalar(nwin, counts, P / 2 - 0.5, 1.0 / P, ALU.add, ALU.mult)
            did_read(dve.tensor_tensor(slot_e, ranks, off9[:, 0:NE].unsqueeze(1).to_broadcast([P, NB, NE]), ALU.add),
                     ("route",))
            after_read(dve, ("route",))
            link(dve.tensor_tensor(slot_e, slot_e, hot, ALU.mult))
            link(dve.tensor_reduce(slot, slot_e, AX, ALU.add))
            link(dve.tensor_tensor(slot_k, slot.unsqueeze(2).to_broadcast([P, NB, NB]),
                                   table("blocks").unsqueeze(1).to_broadcast([P, NB, NB]), ALU.subtract))
            dve.tensor_tensor(onehot.rearrange("p b (k s) -> p b k s", k=NB),
                              table("iota").unsqueeze(1).unsqueeze(1).to_broadcast([P, NB, NB, P]),
                              slot_k.unsqueeze(3).to_broadcast([P, NB, NB, P]), ALU.is_equal).then_inc(onehot_ready, 1)
            link(dve.tensor_scalar(nwin, nwin, ROUND, None, ALU.add))
            link(dve.tensor_scalar(nwin, nwin, ROUND, None, ALU.subtract))
            link(dve.tensor_tensor(cum_prod, before, nwin.unsqueeze(1).to_broadcast([P, NE + 1, NE]), ALU.mult))
            link(dve.tensor_reduce(cum9, cum_prod, AX, ALU.add))
            dve.tensor_copy(win_i, cum9).then_inc(windows_ready, 1)
            dve.tensor_copy(off_i, off9[:, 0:NE]).then_inc(windows_ready, 1)
            dve.tensor_copy(row_i, slot).then_inc(rows_ready, 1)

            one_ahead = [*h_copied, *t_filled, *h_ready, y_copied, y_added]
            for i, s in enumerate(one_ahead + 2 * (h_filled + o_done)):
                dve.memset(spare[:, i:i + 1], 0.0).then_inc(s, 1)

            dve.wait_ge(lexp_ready, 1)
            link(dve.tensor_reduce(psum_e, lexp, AX, ALU.add))
            link(dve.reciprocal(prob, psum_e))
            dve.memset(xs_t[:, :, NB * P:], 0.0).then_inc(pad_ready, 1)
            for c in range(1, DCH, 2):
                sorted_tokens(dve, c, dve.tensor_copy)

            for c in range(DCH):
                after_read(dve, ("xs", c))
            dve.wait_ge(pad_ready, 1)
            dve.wait_ge(windows_ready, 2)
            bounds = [dve.value_load(win_i[0:1, e:e + 1], min_val=0, max_val=MAXW) for e in range(NE + 1)]
            offsets = [dve.value_load(off_i[0:1, e:e + 1], min_val=0, max_val=NB * P) for e in range(NE)]
            dve.wait_ge(bias_loaded, 16)
            for e in range(NE):
                with dve.If(bounds[e] < bounds[e + 1]):
                    with dve.Fori(bounds[e], bounds[e + 1]) as w:
                        first_row = window_row(offsets[e], w - bounds[e])
                        dve.tensor_copy(x_win, xs_t[:, :, bass.ds(first_row, P)]).then_inc(xw_ready, 1)
                        for k in range(2):
                            hidden_may_copy(dve, 1, w, k)
                            dve.tensor_copy(hid[1], bank[:, H_BANK[1], :]).then_inc(h_copied[1], 1)
                            dve.wait_ge(t_filled[1], 2 * w + k + 2)
                            dve.wait_ge(o_done[1], 2 * w + k + 2)
                            for i in range(HB_CH):
                                m = HB_CH * (2 * k + 1) + i
                                ins = dve.tensor_scalar(hid_t[:, 1, i, :], bank[:, T_BANK[1], i * P:(i + 1) * P],
                                                        b1_sb[:, e, m:m + 1], 0.0, ALU.add, ALU.max)
                            ins.then_inc(h_ready[1], 1)

            for b in range(NB):
                dve.wait_ge(gathered[b], 16)
                dve.scalar_tensor_tensor(out=x_sb[:, b, :], in0=y_tok[:, b, :], scalar=prob[:, b:b + 1],
                                         in1=x_sb[:, b, :], op0=ALU.mult, op1=ALU.add).then_inc(result_ready, 1)

        @block.gpsimd
        def _(pool):
            steps = [0]

            def link(ins):
                steps[0] += 1
                ins.then_inc(pool_step, 1)
                pool.wait_ge(pool_step, steps[0])

            def inverse_root(k):
                pool.wait_ge(var_ready, k)
                pool.tensor_tensor(rstd, var_eps, m_half, ALU.pow).then_inc(rstd_ready, 1)

            pool.wait_ge(half_ready, 1)
            inverse_root(1)
            pool.wait_ge(tab_loaded, 16)
            pool.wait_ge(dt_ready, 2)
            pool.wait_ge(step_ph_ready, 1)
            for i in range(2 * BL // 2):
                dst, r = (b_sin1, b_sin2)[i // 4], 2 * (i % 4)
                turns = dst[:, r:r + 2, :]
                for k in (r, r + 1):
                    ins = pool.tensor_scalar(dst[:, k, :], dt_sb, step_ph[:, AH + k:AH + k + 1],
                                             table("phase")[:, 1 + i // 4:2 + i // 4], ALU.mult, ALU.add)
                link(ins)
                link(pool.tensor_scalar(round_g, turns, ROUND, 1.0, ALU.add, ALU.mult))
                link(pool.tensor_scalar(round_g, round_g, -ROUND, 1.0, ALU.add, ALU.mult))
                pool.tensor_tensor(turns, round_g, turns, ALU.subtract).then_inc(b_phase_ready, 1)
            pool.wait_ge(b_phase_ready, 2 * BL // 2)
            pool.memset(y_out, 0.0).then_inc(zeros_ready, 1)
            pool.wait_ge(zeros_ready, 1)
            pool.dma_start(y_rows[NB * P:, :], y_out).then_inc(rows_sent, 16)
            pool.wait_ge(b_sin_ready, 2)
            pool.wait_ge(wri_loaded, 16)
            pool.tensor_tensor(b_sin1, b_sin1, wri[:, 0, :].unsqueeze(1).to_broadcast([P, BL, D]), ALU.mult) \
                .then_inc(wr_done, 1)
            for k in range(2 * NB):
                inverse_root(k + 2)

            pool.wait_ge(windows_ready, 2)
            bounds = [pool.value_load(win_i[0:1, e:e + 1], min_val=0, max_val=MAXW) for e in range(NE + 1)]
            offsets = [pool.value_load(off_i[0:1, e:e + 1], min_val=0, max_val=NB * P) for e in range(NE)]
            for e in range(NE):
                pool.wait_ge(b2_loaded[e % NB2], 16 * (e // NB2 + 1))
                with pool.If(bounds[e] < bounds[e + 1]):
                    with pool.Fori(bounds[e], bounds[e + 1]) as w:
                        first_row = window_row(offsets[e], w - bounds[e])
                        pool.wait_ge(y_copied, w + 2)
                        pool.wait_ge(rows_sent, 16 * w + 16)
                        pool.tensor_tensor(y_out, y_raw, b2_sb[e % NB2], ALU.add).then_inc(y_added, 1)
                        pool.wait_ge(y_added, w + 2)
                        pool.dma_start(y_rows[bass.ds(first_row, P), :], y_out).then_inc(rows_sent, 16)
            pool.wait_ge(rows_sent, 16 * bounds[NE] + 16)
            pool.tensor_tensor(rstd, m_half, m_half, ALU.mult)
            pool.wait_ge(rows_ready, 1)
            for b in range(NB):
                pool.indirect_dma_start(y_tok[:, b, :], None, y_rows,
                                        bass.IndirectOffsetOnAxis(ap=row_i[:, b:b + 1], axis=0)) \
                    .then_inc(gathered[b], 16)

        @block.tensor
        def _(pe):
            def col_slice(c):
                return slice(c * P, (c + 1) * P)

            pe.wait_ge(qk_loaded, 48)
            for d in range(DCH):
                dst = may_fill(pe, ("wqk", d))
                for e in range(DCH):
                    pe.matmul(dst[:, 0:DC], wq_sb[:, e, col_slice(d)], wk_sb[:, e, :], start=e == 0, stop=e == DCH - 1)
                for e in range(DCH):
                    ins = pe.matmul(dst[:, DC:DC + 1], wq_sb[:, e, col_slice(d)], bkq_sb[:, e, 0:1],
                                    start=e == 0, stop=e == DCH - 1)
                did_fill(ins, ("wqk", d))
            dst = may_fill(pe, ("bias",))
            for c in range(CCH):
                for e in range(DCH):
                    pe.matmul(dst[:, c:c + 1], wk_sb[:, e, col_slice(c)], bkq_sb[:, e, 1:2],
                              start=e == 0, stop=e == DCH - 1)
            pe.wait_ge(tab_loaded, 16)
            pe.wait_ge(bkq_ready, 1)
            did_fill(pe.matmul(dst[:, 2:3], ones, bkq_sum, start=True, stop=True), ("bias",))
            pe.wait_ge(xn1_ready, 1)
            for b in range(NB):
                dst = may_fill(pe, ("xnT", b))
                for c in range(DCH):
                    ins = pe.transpose(dst[:, col_slice(c)], xn1[:, b, col_slice(c)], ident)
                did_fill(ins, ("xnT", b))
            for d in range(DCH):
                after_read(pe, ("wqk", d))
            for b in range(NB):
                after_read(pe, ("xnT", b))
            for c in range(CCH):
                dst = may_fill(pe, ("q", c))
                for d in range(DCH):
                    ins = pe.matmul(dst, wqk[:, d, col_slice(c)], xn1_t[:, d, :], start=d == 0, stop=d == DCH - 1)
                did_fill(ins, ("q", c))
            dst = may_fill(pe, ("qb",))
            for b in range(NB):
                for d in range(DCH):
                    ins = pe.matmul(dst[:, b:b + 1], xn1_t[:, d, col_slice(b)], wqb[:, d:d + 1],
                                    start=d == 0, stop=d == DCH - 1)
            did_fill(ins, ("qb",))

            def turn_context(b, j):
                if j == 0:
                    pe.wait_ge(place_loaded[b], 16)
                for c in range(CCH):
                    dst = may_fill(pe, ("ct", b, j, c))
                    for k in range(KPQ):
                        ins = pe.transpose(dst[:, col_slice(k)], ctx_sb[b][:, KPQ * j + k, col_slice(c)], ident)
                    did_fill(ins, ("ct", b, j, c))

            def scores(b, j):
                dst = may_fill(pe, ("s", b, j))
                for c in range(CCH):
                    if b == 0 and j == 0:
                        after_read(pe, ("q", c))
                    after_read(pe, ("ct", b, j, c))
                    ins = pe.matmul(dst, q_t[:, c, col_slice(b)], ctx_t[:, j % 2, c, :], start=c == 0, stop=c == CCH - 1)
                did_fill(ins, ("s", b, j))

            def turn_probs(b, j):
                after_read(pe, ("s", b, j))
                dst = may_fill(pe, ("pT", b, j))
                for k in range(KPQ):
                    ins = pe.transpose(dst[:, col_slice(k)], probs[:, col_slice(KPQ * j + k)], ident)
                did_fill(ins, ("pT", b, j))

            def probs_context(b):
                dst = may_fill(pe, ("pv", b))
                for j in range(NQ):
                    after_read(pe, ("pT", b, j))
                    for k in range(KPQ * j, KPQ * j + KPQ):
                        ins = pe.matmul(dst[:, 0:DC], probs_t[:, k, :], ctx_sb[b][:, k, :],
                                        start=k == 0, stop=k == KCH - 1)
                did_fill(ins, ("pv", b))

            def kernel_products():
                pe.wait_ge(a_tab_ready, 1)
                pe.wait_ge(b_tab_ready, 1)
                a_cols = a_tab.rearrange("p a (h g) -> p (a h) g", h=HG)
                b_cols = b_tab.rearrange("p b (h g) -> p (b h) g", h=HG)
                for g in range(8):
                    dst = may_fill(pe, ("k1", g))
                    for i in range(8):
                        ins = pe.matmul(dst[:, i * BL * HG:(i + 1) * BL * HG], a_cols[:, :, 8 * g + i],
                                        b_cols[:, :, 8 * g + i], start=True, stop=True)
                    did_fill(ins, ("k1", g))
                dst = may_fill(pe, ("k2",))
                after_read(pe, ("k1", 6))
                after_read(pe, ("k1", 7))
                pick = table("pick")
                for i in range(BL):
                    ins = pe.matmul(dst, pick[:, BL - 1 - i:BL - 1 - i + P], k_parts[:, i, :],
                                    start=i == 0, stop=i == BL - 1)
                did_fill(ins, ("k2",))
                after_read(pe, ("k2",))
                for i in range(2):
                    dst = may_fill(pe, ("k3", i))
                    did_fill(pe.matmul(dst, table(("cos_f", "sin_f")[i]), k_time, start=True, stop=True), ("k3", i))

            def values(b):
                dst = may_fill(pe, ("anT", b))
                after_read(pe, ("pv", b))
                for c in range(CCH):
                    ins = pe.transpose(dst[:, col_slice(c)], an[:, col_slice(c)], ident)
                did_fill(ins, ("anT", b))
                dst = may_fill(pe, ("av", b))
                pe.wait_ge(wv_loaded, 16)
                after_read(pe, ("anT", b))
                for c in range(CCH):
                    ins = pe.matmul(dst, an_t[:, c, :], wv_sb[:, c, :], start=c == 0, stop=c == CCH - 1)
                did_fill(ins, ("av", b))

            def to_frequency(b):
                pe.wait_ge(u_ready, b + 1)
                for what, name in ((("uc", b), "cos_f"), (("us", b), "sin_f")):
                    dst = may_fill(pe, what)
                    did_fill(pe.matmul(dst, table(name), u_sb, start=True, stop=True), what)

            def to_time(b):
                pe.wait_ge(spec_ready, b + 1)
                dst = may_fill(pe, ("y", b))
                pe.matmul(dst, table("cos_t"), y_cos, start=True, stop=False)
                did_fill(pe.matmul(dst, table("sin_t"), y_sin, start=False, stop=True), ("y", b))

            def gate(b):
                pe.wait_ge(xn2_ready, b + 1)
                dst = may_fill(pe, ("x2T", b))
                for c in range(DCH):
                    ins = pe.transpose(dst[:, col_slice(c)], xn2[:, b, col_slice(c)], ident)
                did_fill(ins, ("x2T", b))
                dst = may_fill(pe, ("lg", b))
                pe.wait_ge(gate_loaded, 32)
                after_read(pe, ("x2T", b))
                for c in range(DCH):
                    ins = pe.matmul(dst[:, 0:NE], xn2_t[:, c, :], wg_sb[:, c, :], start=c == 0, stop=c == DCH - 1)
                did_fill(ins, ("lg", b))

            for j in range(NQ):
                turn_context(0, j)
                scores(0, j)
            for b in range(NB):
                for j in range(NQ):
                    turn_probs(b, j)
                    if b + 1 < NB:
                        turn_context(b + 1, j)
                        scores(b + 1, j)
                if b == 1:
                    kernel_products()
                if b >= 1:
                    values(b - 1)
                if b >= 2:
                    to_time(b - 2)
                probs_context(b)
                if b >= 1:
                    to_frequency(b - 1)
                if b >= 2:
                    gate(b - 2)
            values(3)
            to_time(2)
            to_frequency(3)
            gate(2)
            to_time(3)
            gate(3)

            dst = may_fill(pe, ("route",))
            pe.wait_ge(hot_ready, 1)
            for b in range(NB):
                for s in range(b + 1):
                    pe.matmul(dst[:, b * NE:(b + 1) * NE], ones if s < b else table("earlier"), hot[:, s, :],
                              start=s == 0, stop=s == b)
            for s in range(NB):
                ins = pe.matmul(dst[:, NB * NE:NB * NE + NE], ones, hot[:, s, :], start=s == 0, stop=s == NB - 1)
            did_fill(ins, ("route",))

            pe.wait_ge(onehot_ready, 1)
            for c in range(DCH):
                dst = may_fill(pe, ("xs", c))
                for b in range(NB):
                    ins = pe.matmul(dst, xn2[:, b, col_slice(c)], onehot[:, b, :], start=b == 0, stop=b == NB - 1)
                did_fill(ins, ("xs", c))

            def weights(e, u):
                j = UNITS * e + u
                pe.wait_ge(place_loaded[weight_place(j)], 16 * weight_count(j))
                return ring[:, weight_place(j), :]

            def hidden(e, w, i):
                parity, k = i % 2, i // 2
                w1_half = weights(e, k).rearrange("p (d m) -> p d m", d=DCH)
                pe.wait_ge(h_copied[parity], 2 * w + k + 1)
                for d in range(DCH):
                    ins = pe.matmul(bank[:, H_BANK[parity], :], x_win[:, d, :], w1_half[:, d, parity * 512:(parity + 1) * 512],
                                    start=d == 0, stop=d == DCH - 1)
                ins.then_inc(h_filled[parity], 1)

            def turn_hidden(w, i):
                parity, k = i % 2, i // 2
                pe.wait_ge(h_copied[parity], 2 * w + k + 2)
                pe.wait_ge(h_ready[parity], 2 * w + k + 1)
                for c in range(HB_CH):
                    ins = pe.transpose(bank[:, T_BANK[parity], col_slice(c)], hid[parity][:, col_slice(c)], ident)
                ins.then_inc(t_filled[parity], 1)

            def output(e, w, i):
                parity, k = i % 2, i // 2
                w2_half = weights(e, 2 + k).rearrange("p (m n) -> p m n", m=8)
                pe.wait_ge(h_ready[parity], 2 * w + k + 2)
                for c in range(HB_CH):
                    m = HB_CH * i + c
                    ins = pe.matmul(bank[:, Y_BANK, :], hid_t[:, parity, c, :], w2_half[:, m % 8, :], start=m == 0,
                                    stop=m == MCH - 1)
                ins.then_inc(o_done[parity], 1)

            for b in range(8):
                pe.wait_ge(drained[b], FILL_COUNT[b])
            pe.wait_ge(windows_ready, 2)
            bounds = [pe.value_load(win_i[0:1, e:e + 1], min_val=0, max_val=MAXW) for e in range(NE + 1)]
            for e in range(NE):
                with pe.If(bounds[e] < bounds[e + 1]):
                    with pe.Fori(bounds[e], bounds[e + 1]) as w:
                        pe.wait_ge(xw_ready, w + 1)
                        hidden(e, w, 0)
                        hidden(e, w, 1)
                        turn_hidden(w, 0)
                        hidden(e, w, 2)
                        turn_hidden(w, 1)
                        pe.wait_ge(y_copied, w + 1)
                        output(e, w, 0)
                        hidden(e, w, 3)
                        turn_hidden(w, 2)
                        output(e, w, 1)
                        turn_hidden(w, 3)
                        output(e, w, 2)
                        output(e, w, 3)


def shape_tables():
    import numpy as np

    t = np.zeros((P, TABLE_COLS), np.float32)

    def put(name, value):
        lo, hi = TABLES[name]
        t[:, lo:hi] = value

    p = np.arange(P)
    angle = np.pi * (((2 * p[None, :] + 1) * p[:, None]) % (4 * P)) / (2 * P)
    put("ident", np.eye(P))
    put("ones", 1.0)
    put("cos_f", np.cos(angle))
    put("sin_f", np.sin(angle))
    put("cos_t", np.cos(angle.T) / P)
    put("sin_t", np.sin(angle.T) / P)
    put("pick", np.arange(P + BL - 1)[None, :] == (BL * (p // HG) + BL - 1)[:, None])
    put("own", np.arange(HG)[None, :] == (p % HG)[:, None])
    put("earlier", p[:, None] < p[None, :])
    put("iota", np.arange(P))
    put("blocks", P * np.arange(NB))
    put("rank_e", NE - np.arange(NE))
    put("before_e", (np.arange(NE)[None, :] < np.arange(NE + 1)[:, None]).ravel())
    put("steps", np.concatenate([BL * np.arange(AH), np.arange(BL)]))
    put("phase", np.where(p[:, None] < NS, [[0.25, 0.25, 0.5]], [[0.0, 0.5, 0.75]]))
    return t


def kernel(**inputs):
    import numpy as np
    import concourse.bacc as bacc
    from concourse.bass_utils import run_bass_kernel_spmd

    g = {k: np.asarray(v) for k, v in inputs.items()}
    nc = bacc.Bacc("TRN2", target_bir_lowering=False, num_devices=1)
    w_re_t, w_im_t = g["L0_attn_W_re"].T, g["L0_attn_W_im"].T
    lam = np.stack([g["L0_attn_Lambda_re"], g["L0_attn_Lambda_im"]], 1)
    arrays = {
        "x": g["x"].reshape(NB * LQ, D),
        "ctx": g["ctx_512"],
        "wq_t": g["L0_xattn_Wq"].T,
        "wk_t": g["L0_xattn_Wk"].T,
        "bkq": np.stack([g["L0_xattn_bk"], g["L0_xattn_bq"]], 1),
        "wv": g["L0_xattn_Wv"],
        "bv": g["L0_xattn_bv"],
        "log_dt": g["L0_attn_log_dt"],
        "w_ri": np.stack([np.concatenate([w_re_t, w_re_t]), np.concatenate([w_im_t, w_im_t])]),
        "lam": np.concatenate([lam, lam]),
        "d_skip": g["L0_attn_D"].reshape(1, D),
        "w_gate": g["L0_ffn_w_gate"],
        "b_gate": g["L0_ffn_b_gate"],
        "w1": g["L0_ffn_W1"],
        "b1": g["L0_ffn_b1"].reshape(NE, MCH, P).transpose(2, 0, 1),
        "w2": g["L0_ffn_W2"],
        "b2": g["L0_ffn_b2"],
        "tables": shape_tables(),
    }
    arrays = {f"in_{k}": np.ascontiguousarray(v) for k, v in arrays.items()}
    args = [nc.dram_tensor(k, v.shape, mybir.dt.from_np(v.dtype), kind="ExternalInput").ap()
            for k, v in arrays.items()]
    out = nc.dram_tensor("out", (NB * LQ, D), F32, kind="ExternalOutput").ap()
    perceiver_layer(nc, *args, out)
    r = run_bass_kernel_spmd(nc, [arrays], core_ids=[0])
    return r.results[0]["out"].reshape(NB, LQ, D)
```

```python
from contextlib import ExitStack

import concourse.bass as bass
from concourse import mybir

F32 = mybir.dt.float32
F32R = mybir.dt.float32r
I32 = mybir.dt.int32
U32 = mybir.dt.uint32
ALU = mybir.AluOpType
ACT = mybir.ActivationFunctionType
AX = mybir.AxisListType.X

P = 128
NB, LQ, D = 4, 128, 512
LK, DC = 2048, 256
NS = 64
NE, DM = 8, 2048
DCH, CCH, MCH = D // P, DC // P, DM // P
KCH = LK // P
NQ = 4
KPQ = KCH // NQ
AH, BL = 16, 8
B_POOL = 4
HG = P // AH
MAXW = NE + (NB * LQ - NE) // P
HB_CH = 4
NB2 = 2
NSLOT = 8
NSPLIT = 4
BLOCKS = (("h", 0), ("h", 1), ("h", 2), ("o", 0), ("h", 3), ("o", 1), ("o", 2), ("o", 3))
PARTS = 2 * len(BLOCKS)
LOW_BY_GPSIMD = (6, 12, 13, 15)
UNITS = 4
EPS = 1e-5
ROUND = 1.5 * 2.0 ** 23
TWO_PI = 6.283185307179586

TABLES = {}
_at = 0
for _name, _n in (("ident", P), ("ones", P), ("cos_f", P), ("sin_f", P), ("cos_t", P), ("sin_t", P),
                  ("pick", P + BL - 1), ("own", HG), ("earlier", P), ("iota", P), ("blocks", NB), ("rank_e", NE),
                  ("before_e", (NE + 1) * NE)):
    TABLES[_name] = (_at, _at + _n)
    _at += _n
TABLE_COLS = _at
COLS = 171

S_BANK = [0, 1, 2, 3]
T0, T1, T2, O_BANK = 4, 5, 6, 7
H_BANK, T_BANK, Y_BANK = (4, 5), (6, 7), 0

FILLS = [(S_BANK[d], ("wqk", d)) for d in range(DCH)] + [(O_BANK, ("bias",))]
FILLS += [((T0, T1, T2, T0)[b], ("xnT", b)) for b in range(NB)]
FILLS += [(S_BANK[c], ("q", c)) for c in range(CCH)] + [(O_BANK, ("qb",))]


def _context_fills(b, j):
    return [(T0, ("ct", b, j, 0)), (T1, ("ct", b, j, 1))]


def _score_fills(b, j):
    return (_context_fills(b, j + 1) if j + 1 < NQ else []) + [(S_BANK[j], ("s", b, j))]


def _kernel_fills():
    out = [((T0, T1)[g % 2], ("k1", g)) for g in range(8)]
    return out + [(T2, ("k2",)), (T0, ("k3", 0)), (T1, ("k3", 1))]


def _value_fills(b):
    return [(S_BANK[0] if b == NB - 1 else T2, ("anT", b)), (T0, ("av", b))]


def _freq_fills(b):
    return [(T1, ("uc", b)), (O_BANK, ("us", b))]


def _time_fills(b):
    return [(T0, ("y", b))]


def _gate_fills(b):
    return [(T1, ("x2T", b)), (T2, ("lg", b))] if b == 0 else [(S_BANK[1], ("x2T", b)), (S_BANK[2], ("lg", b))]


FILLS += _context_fills(0, 0)
for _j in range(NQ):
    FILLS += _score_fills(0, _j)
FILLS += _context_fills(1, 0)
for _b in range(NB):
    for _j in range(NQ):
        FILLS.append((T2 if _b + 1 < NB else (T2, T1, T0, T1)[_j], ("pT", _b, _j)))
        if _b + 1 < NB:
            FILLS += _score_fills(_b + 1, _j)
    if _b + 2 < NB:
        FILLS += _context_fills(_b + 2, 0)
    if _b >= 1:
        FILLS += _value_fills(_b - 1)
    if _b >= 2:
        FILLS += _time_fills(_b - 2)
    FILLS.append((O_BANK, ("pv", _b)))
    if _b == 1:
        FILLS += _kernel_fills()
    if _b >= 1:
        FILLS += _freq_fills(_b - 1)
    if _b == 2:
        FILLS += _gate_fills(0)
FILLS += (_value_fills(3) + _gate_fills(1) + _time_fills(2) + _freq_fills(3) + _gate_fills(2) + _time_fills(3)
          + _gate_fills(3) + [(T0, ("route",))] + [(S_BANK[c], ("xs", c)) for c in range(DCH)])

FILL_NO = {}
FILL_COUNT = [0] * 8
for _bank, _what in FILLS:
    FILL_COUNT[_bank] += 1
    FILL_NO[_what] = (_bank, FILL_COUNT[_bank])


def perceiver_layer(nc, x, ctx, wq_t, wk_t, bkq, wv, bv, log_dt, w_ri, lam, d_skip,
                    w_gate, b_gate, w1, b1, w2, b2, times, tables, out):
    x_rows = x.rearrange("(b t) h -> t b h", t=P)
    out_rows = out.rearrange("(b t) h -> t b h", t=P)
    y_rows = nc.dram_tensor("y_rows", ((NB + 1) * P, D), F32, kind="Internal").ap()

    with ExitStack() as stack:
        def sb(name, shape, dt=F32):
            return stack.enter_context(nc.sbuf_tensor(name, shape, dt))

        def sem(name):
            return stack.enter_context(nc.semaphore(name))

        bank = stack.enter_context(nc.psum_tensor("bank", [P, 8, 512], F32))

        def next_at():
            return -(-nc.sbuf_base // 32) * 32

        ring_at = next_at()
        ring = sb("ring", [P, NSLOT + 2, 4096])
        x_sb = sb("x_sb", [P, NB, D])
        work_at = next_at()
        work = sb("work", [P, 4096])
        hbuf_at = next_at()
        hbuf = sb("hbuf", [P, 1024])
        late = sb("late", [P, 5 * D])
        kfreq = late[:, 0:2 * D].rearrange("p (k h) -> p k h", k=2)
        wri = late[:, 2 * D:4 * D].rearrange("p (k h) -> p k h", k=2)
        dt_sb = late[:, 4 * D:5 * D]
        xs_t = late[:].rearrange("p (c n) -> p c n", c=DCH)
        small = sb("small", [P, 1024])
        tab = sb("tab", [P, TABLE_COLS])
        cols = sb("cols", [P, COLS])
        icols = sb("icols", [P, 24], I32)

        def table(name):
            lo, hi = TABLES[name]
            return tab[:, lo:hi]

        ident, ones = table("ident"), table("ones")

        ctx_sb = [ring[:, b, :].rearrange("p (k c) -> p k c", k=KCH) for b in range(NB)]
        a_sin = ring[:, 2:4, :].rearrange("p s (a h) -> p (s a) h", h=D)
        a_tab = ring[:, 6:8, :].rearrange("p s (a h) -> p (s a) h", h=D)
        b_tab = ring[:, 4, :].rearrange("p (b h) -> p b h", h=D)
        b_sin1 = ring[:, 5, :].rearrange("p (b h) -> p b h", h=D)
        k_parts = ring[:, 5, :].rearrange("p (b h) -> p b h", h=D)
        b_sin2 = work[:].rearrange("p (b h) -> p b h", h=D)
        xn2 = work[:, 0:2048].rearrange("p (b h) -> p b h", h=D)
        y_cos, y_sin, prod1, prod2 = (work[:, 2048 + i * D:2560 + i * D] for i in range(4))
        scratch = ring[:, 8:10, :].rearrange("p s n -> p (s n)")
        xn1 = scratch[:, 0:2048].rearrange("p (b h) -> p b h", h=D)
        probs = scratch[:, 0:2048]
        xn1_t = scratch[:, 2048:4096].rearrange("p (c n) -> p c n", c=DCH)
        probs_t = scratch[:, 2048:4096].rearrange("p (k n) -> p k n", k=KCH)
        wq_sb = scratch[:, 4096:6144].rearrange("p (e d) -> p e d", e=DCH)
        ctx_t = scratch[:, 4096:6144].rearrange("p (u c n) -> p u c n", u=2, c=CCH)
        wk_sb = scratch[:, 6144:7168].rearrange("p (e c) -> p e c", e=DCH)
        q_t = scratch[:, 6144:7168].rearrange("p (c n) -> p c n", c=CCH)
        wqk = scratch[:, 7168:8192].rearrange("p (d c) -> p d c", d=DCH)
        bv_sb = kfreq[:, 0, :]
        u_sb = wri[:, 0, :]
        xn2_t = wri[:, 1, :].rearrange("p (c n) -> p c n", c=DCH)
        an = dt_sb[:, 0:DC]
        an_t = dt_sb[:, DC:2 * DC].rearrange("p (c n) -> p c n", c=CCH)
        round_v = hbuf[:].rearrange("p (a h) -> p a h", h=D)
        wv_sb = hbuf[:].rearrange("p (c n) -> p c n", c=CCH)
        round_g = small[:].rearrange("p (a h) -> p a h", h=D)
        k_time = small[:, 0:D]
        b1_sb = small[:, 0:NE * MCH].rearrange("p (e c) -> p e c", e=NE)
        y_out = small[:, 512:1024]
        b2_sb = [work[:, i * D:(i + 1) * D] for i in range(NB2)]
        hid = [work[:, 2048 + i * D:2560 + i * D] for i in range(2)]
        y_tok = xn2

        w_hi = nc.alloc_sbuf_tensor_at("w_hi", [P, NSPLIT, 2, 512], F32R, offset=ring_at + NSLOT * 16384)
        w_lo = nc.alloc_sbuf_tensor_at("w_lo", [P, NSPLIT, 2, 512], F32R, offset=ring_at + (NSLOT + 1) * 16384)
        x_hi = nc.alloc_sbuf_tensor_at("x_hi", [P, DCH, P], F32R, offset=work_at + 3072 * 4)
        x_lo = nc.alloc_sbuf_tensor_at("x_lo", [P, DCH, P], F32R, offset=work_at + 3584 * 4)

        h_hi = nc.alloc_sbuf_tensor_at("h_hi", [P, 2, HB_CH, P], F32R, offset=hbuf_at)
        h_lo = nc.alloc_sbuf_tensor_at("h_lo", [P, 2, HB_CH, P], F32R, offset=work_at + 1024 * 4)
        xn2_hi = [w_hi[:, 2 + b // 2, b % 2, :] for b in range(NB)]
        xn2_lo = [w_lo[:, 2 + b // 2, b % 2, :] for b in range(NB)]
        onehot = nc.alloc_sbuf_tensor_at("onehot", [P, NB, D], F32R, offset=work_at)

        _next = [0]

        def col(n):
            _next[0] += n
            assert _next[0] <= COLS
            return cols[:, _next[0] - n:_next[0]]

        lam_c, decay, times_c = col(2), col(1), col(AH + BL + 3)
        step_l, phase_c = times_c[:, 0:AH + BL], times_c[:, AH + BL:]
        step_mag, step_ph = col(AH + BL), col(AH + BL)
        bn6, mv = col(6), col(2 * NB)
        rstd, var_eps, m_half = col(NB), col(NB), col(NB)
        bkq_sb = col(2 * DCH).rearrange("p (e k) -> p e k", k=2)
        bkq_prod, bkq_sum = col(DCH), col(1)
        qbias, wqb, q_bk = col(3), col(DCH), col(NB)
        row_stats, nbias = col(2 * NB * NQ), col(NB)
        qmax, rsum = row_stats[:, 0:NB * NQ], row_stats[:, NB * NQ:]
        rmax, rmax_q, rtot = col(1), col(1), col(1)
        spare = row_stats
        logits = tab[:, TABLES["pick"][0]:TABLES["pick"][0] + NB * NE].rearrange("p (b e) -> p b e", e=NE)
        rt0 = TABLES["cos_f"][0]

        def route(i, n):
            return tab[:, rt0 + i:rt0 + i + n]

        lmax = route(0, 4)
        lsub = route(4, 32).rearrange("p (b e) -> p b e", e=NE)
        first = route(36, 32).rearrange("p (b e) -> p b e", e=NE)
        hot_2d = route(68, 32)
        hot = hot_2d.rearrange("p (b e) -> p b e", e=NE)
        fmax = route(100, 4)
        psum_e, prob = route(104, 4), route(108, 4)
        rt1 = TABLES["sin_f"][0]
        lexp = tab[:, rt1:rt1 + 32].rearrange("p (b e) -> p b e", e=NE)
        nwin = tab[:, rt1 + 32:rt1 + 40]
        cum9 = tab[:, rt1 + 40:rt1 + 49]
        slot_e = tab[:, rt1 + 57:rt1 + 89].rearrange("p (b e) -> p b e", e=NE)
        slot = tab[:, rt1 + 89:rt1 + 93]
        rt2 = TABLES["cos_t"][0]
        cum_prod = tab[:, rt2:rt2 + 72].rearrange("p (e f) -> p e f", f=NE)
        slot_k = tab[:, rt2 + 72:rt2 + 88].rearrange("p (b k) -> p b k", b=NB)
        off9 = tab[:, rt2 + 88:rt2 + 97]
        rt3 = TABLES["sin_t"][0]
        seq_before = tab[:, rt3:rt3 + (NB + 1) * NE].rearrange("p (b e) -> p b e", e=NE)
        win_i = icols[:, 0:NE + 1]
        off_i = icols[:, 9:17]
        row_i = icols[:, 17:21].bitcast(U32)
        wg_sb = sb("wg_sb", [P, DCH, NE])
        bg_sb = sb("bg_sb", [P, NE])
        d_sb = kfreq[0:1, 1, :]

        filled = [sem(f"bank{k}_filled") for k in range(8)]
        drained = [sem(f"bank{k}_drained") for k in range(8)]
        place_loaded = [sem(f"place{k}_loaded") for k in range(NSLOT)]
        params_loaded, tab_loaded, x_loaded = sem("params_loaded"), sem("tab_loaded"), sem("x_loaded")
        qk_loaded, bv_loaded, wri_loaded = sem("qk_loaded"), sem("bv_loaded"), sem("wri_loaded")
        wv_loaded, gate_loaded, d_loaded = sem("wv_loaded"), sem("gate_loaded"), sem("d_loaded")
        bias_loaded = sem("bias_loaded")
        b2_loaded = [sem(f"b2_{i}_loaded") for i in range(NB2)]
        dve_step = sem("dve_step")
        pool_step = sem("pool_step")
        dt_ready, step_mag_ready, step_ph_ready = sem("dt_ready"), sem("step_mag_ready"), sem("step_ph_ready")
        half_ready, zeros_ready, mags_ready = sem("half_ready"), sem("zeros_ready"), sem("mags_ready")
        a_phase_ready, b_phase_ready = sem("a_phase_ready"), sem("b_phase_ready")
        turns_ready = sem("turns_ready")
        b_phase_end_ready = sem("b_phase_end_ready")
        a_sin_ready, b_sin_ready = sem("a_sin_ready"), sem("b_sin_ready")
        wr_done, wi_done, b_sum_ready = sem("wr_done"), sem("wi_done"), sem("b_sum_ready")
        a_tab_ready, b_tab_ready = sem("a_tab_ready"), sem("b_tab_ready")
        var_ready, rstd_ready = sem("var_ready"), sem("rstd_ready")
        xn1_ready, bkq_ready, rmax_ready = sem("xn1_ready"), sem("bkq_ready"), sem("rmax_ready")
        u_ready, spec_ready, xn2_ready = sem("u_ready"), sem("spec_ready"), sem("xn2_ready")
        xn2_hi_ready, xn2_lo_ready = sem("xn2_hi_ready"), sem("xn2_lo_ready")
        hot_ready, lsub_ready, lexp_ready = sem("hot_ready"), sem("lsub_ready"), sem("lexp_ready")
        windows_ready, rows_ready = sem("windows_ready"), sem("rows_ready")
        onehot_ready, pad_ready = sem("onehot_ready"), sem("pad_ready")
        x_hi_ready, xw_ready = sem("x_hi_ready"), sem("xw_ready")
        parts_used = sem("parts_used")
        hi_ready, lo_ready = sem("hi_ready"), sem("lo_ready")
        lo_ready_pool = sem("lo_ready_pool")
        h_copied = [sem(f"h{p}_copied") for p in range(2)]
        t_filled = [sem(f"t{p}_filled") for p in range(2)]
        h_relu = [sem(f"h{p}_relu") for p in range(2)]
        h_hi_ready = [sem(f"h{p}_hi_ready") for p in range(2)]
        h_lo_ready = [sem(f"h{p}_lo_ready") for p in range(2)]
        y_copied, y_added, rows_sent = sem("y_copied"), sem("y_added"), sem("rows_sent")
        gathered = [sem(f"gathered{b}") for b in range(NB)]
        result_ready, result_sent = sem("result_ready"), sem("result_sent")

        def weight_place(j):
            return (4, 5, 6, 7, 0, 1, 2, 3)[j % NSLOT]

        def weight_count(j):
            return j // NSLOT + (2 if weight_place(j) < NB else 1)

        def after_fill(eng, what):
            b, n = FILL_NO[what]
            eng.wait_ge(filled[b], n)

        def after_read(eng, what):
            b, n = FILL_NO[what]
            eng.wait_ge(drained[b], n)

        def may_fill(eng, what):
            b, n = FILL_NO[what]
            if n > 1:
                eng.wait_ge(drained[b], n - 1)
            return bank[:, b, :]

        def did_fill(ins, what):
            ins.then_inc(filled[FILL_NO[what][0]], 1)

        def may_read(eng, what):
            after_fill(eng, what)
            return bank[:, FILL_NO[what][0], :]

        def did_read(ins, what):
            ins.then_inc(drained[FILL_NO[what][0]], 1)

        def sorted_tokens(eng, c, copy):
            src = may_read(eng, ("xs", c))
            did_read(copy(xs_t[:, c, 0:NB * P], src), ("xs", c))

        def window_row(offset, i):
            return nc.s_assert_within(offset + i * P, 0, NB * P,
                                      skip_runtime_bounds_check_because="windows cover only the tokens there are")

        def unit_of(e, n):
            what, i = BLOCKS[n // 2]
            return UNITS * e + (0 if what == "h" else 2) + i // 2

        def weight_part(e, n):
            what, i = BLOCKS[n // 2]
            g = n % 2
            half = ring[:, weight_place(unit_of(e, n)), :]
            if what == "h":
                half = half.rearrange("p (d m) -> p d m", d=DCH)
                return half[:, 2 * g:2 * g + 2, (i % 2) * 512:(i % 2 + 1) * 512]
            m = HB_CH * (i % 2) + 2 * g
            return half.rearrange("p (m n) -> p m n", m=8)[:, m:m + 2, :]

        def wait_block(eng, w, what, i):
            back = i < 0
            n = 2 * BLOCKS.index((what, i % 4)) + 2
            eng.wait_ge(parts_used, PARTS * w + n + (0 if back else PARTS))

        def split_low(eng, e, w, n, done):
            eng.wait_ge(hi_ready, PARTS * w + n + 1)
            eng.tensor_tensor(w_lo[:, n % NSPLIT, :, :], weight_part(e, n), w_hi[:, n % NSPLIT, :, :], ALU.subtract) \
                .then_inc(done, 1)

        def block_may_copy(eng, p, w, k):
            wait_block(eng, w, "h", 2 * k + p)
            eng.wait_ge(h_lo_ready[p], 2 * w + k + 1)

        def block_may_relu(eng, p, w, k):
            eng.wait_ge(t_filled[p], 2 * w + k + 2)

        block = stack.enter_context(nc.Block())

        @block.sync
        def _(sp):
            sp.dma_start(dt_sb, log_dt.partition_broadcast(P)).then_inc(params_loaded, 16)
            sp.dma_start(wk_sb, wk_t.rearrange("(e p) c -> p e c", p=P)).then_inc(qk_loaded, 16)
            sp.dma_start(wq_sb, wq_t.rearrange("(e p) d -> p e d", p=P)).then_inc(qk_loaded, 16)
            sp.dma_start(x_sb[:], x_rows).then_inc(x_loaded, 16)
            sp.dma_start(tab[:], tables).then_inc(tab_loaded, 16)
            for b in range(NB):
                if b == 1:
                    sp.dma_start(wri, w_ri.rearrange("k n h -> n k h")).then_inc(wri_loaded, 16)
                    sp.dma_start(bv_sb, bv.partition_broadcast(P)).then_inc(bv_loaded, 16)
                if b == 2:
                    sp.wait_ge(b_phase_end_ready, (BL - B_POOL) // 2)
                    sp.dma_start(wv_sb, wv.rearrange("(c p) n -> p c n", p=P)).then_inc(wv_loaded, 16)
                    sp.wait_ge(a_tab_ready, 1)
                sp.dma_start(ring[:, b, :], ctx[b].rearrange("(p k) c -> p (k c)", p=P)) \
                    .then_inc(place_loaded[b], 16)

            def load_unit(j):
                e, u = divmod(j, UNITS)
                place = ring[:, weight_place(j), :]
                if u < 2:
                    src = w1[e].rearrange("(d p) m -> p d m", p=P)[:, :, u * 1024:(u + 1) * 1024]
                    dst = place.rearrange("p (d m) -> p d m", d=DCH)
                else:
                    src = w2[e].rearrange("(m p) n -> p m n", p=P)[:, (u - 2) * 8:(u - 1) * 8, :]
                    dst = place.rearrange("p (m n) -> p m n", m=8)
                sp.dma_start(dst, src).then_inc(place_loaded[weight_place(j)], 16)

            for j in range(NSLOT):
                if j == 0:
                    after_fill(sp, ("k1", 7))
                if j == 1:
                    after_fill(sp, ("k2",))
                if 4 <= j < 8:
                    after_fill(sp, ("pv", j - 4))
                load_unit(j)
            sp.wait_ge(windows_ready, 1)
            last = [sp.value_load(win_i[0:1, e + 1:e + 2], min_val=0, max_val=MAXW) for e in range(NE)]

            def load_b2(e):
                sp.dma_start(b2_sb[e % NB2], b2[e].partition_broadcast(P)).then_inc(b2_loaded[e % NB2], 16)

            def next_b2(e):
                sp.wait_ge(y_added, last[e] + 1)
                sp.wait_ge(b2_loaded[e % NB2], 16 * (e // NB2 + 1))
                load_b2(e + NB2)

            after_fill(sp, ("xs", DCH - 1))
            for e in range(NB2):
                load_b2(e)
            for j in range(NSLOT, NE * UNITS):
                e, u = divmod(j - NSLOT, UNITS)
                if u == 0 and e > 0:
                    next_b2(e - 1)
                block = BLOCKS.index(("h" if u < 2 else "o", 2 * (u % 2) + 1))
                sp.wait_ge(parts_used, PARTS * last[e] + 2 * block + 2)
                sp.wait_ge(place_loaded[weight_place(j)], 16 * (weight_count(j) - 1))
                load_unit(j)
            for e in range((NE * UNITS - NSLOT) // UNITS - 1, NE - NB2):
                next_b2(e)
            for b in range(NB):
                sp.wait_ge(result_ready, b + 1)
                sp.dma_start(out_rows[:, b, :], x_sb[:, b, :]).then_inc(result_sent, 16)
            sp.wait_ge(result_sent, 16 * NB)

        @block.scalar
        def _(act):
            act.dma_start(lam_c, lam).then_inc(params_loaded, 16)
            act.dma_start(times_c, times).then_inc(params_loaded, 16)
            act.dma_start(bkq_sb, bkq.rearrange("(e p) k -> p e k", p=P)).then_inc(qk_loaded, 16)
            act.dma_start(wg_sb[:], w_gate.rearrange("(c p) e -> p c e", p=P)).then_inc(gate_loaded, 16)
            act.dma_start(bg_sb[:], b_gate.partition_broadcast(P)).then_inc(gate_loaded, 16)
            act.dma_start(d_sb, d_skip).then_inc(d_loaded, 16)

            act.wait_ge(params_loaded, 48)
            act.activation(decay, lam_c[:, 0:1], ACT.Exp).then_inc(dt_ready, 1)
            act.activation(dt_sb, dt_sb, ACT.Exp).then_inc(dt_ready, 1)

            act.wait_ge(dt_ready, 2)
            act.wait_ge(step_ph_ready, 1)
            for i in range(AH + BL - B_POOL):
                if i < AH:
                    dst, step, shift = a_sin[:, i, :], i, phase_c[:, 0:1]
                else:
                    dst, step, shift = b_sin2[:, i - AH + B_POOL, :], i + B_POOL, phase_c[:, 2:3]
                ins = act.activation(dst, dt_sb, ACT.Identity, scale=step_ph[:, step:step + 1], bias=shift)
                if i % 2:
                    ins.then_inc(turns_ready, 1)

            act.wait_ge(step_mag_ready, 1)
            for i in range(AH + BL):
                dst = a_tab[:, i, :] if i < AH else b_tab[:, i - AH, :]
                ins = act.activation(dst, dt_sb, ACT.Exp, scale=step_mag[:, i:i + 1])
            ins.then_inc(mags_ready, 1)

            def a_sines(i):
                act.wait_ge(a_phase_ready, 2 * i + 2)
                sines = a_sin[:, 4 * i:4 * i + 4, :]
                act.activation(sines, sines, ACT.Sin, scale=-TWO_PI).then_inc(a_sin_ready, 1)

            def b_sines(i):
                if i < 3:
                    act.wait_ge(b_phase_ready, 2 * i + 2)
                else:
                    act.wait_ge(b_phase_end_ready, (BL - B_POOL) // 2)
                sines = (b_sin1, b_sin2)[i // 2][:, 4 * (i % 2):4 * (i % 2) + 4, :]
                act.activation(sines, sines, ACT.Sin, scale=-TWO_PI).then_inc(b_sin_ready, 1)

            a_sines(0)
            b_sines(0)
            a_sines(1)
            b_sines(1)
            after_read(act, ("bias",))
            for c in range(CCH):
                src = may_read(act, ("q", c))
                did_read(act.activation(q_t[:, c, :], src, ACT.Identity, bias=qbias[:, c:c + 1]), ("q", c))
            a_sines(2)
            b_sines(2)
            a_sines(3)
            b_sines(3)

            def softmax_exp(b):
                act.wait_ge(rmax_ready, b + 1)
                for j in range(NQ):
                    if b > 0:
                        after_fill(act, ("pT", b - 1, j))
                    src = may_read(act, ("s", b, j))
                    did_read(act.activation(probs[:, j * 512:(j + 1) * 512], src, ACT.Exp,
                                            bias=nbias[:, b:b + 1], accum_out=rsum[:, NQ * b + j:NQ * b + j + 1]),
                             ("s", b, j))

            def turned_gate_rows(b):
                src = may_read(act, ("x2T", b))
                if b > 0:
                    after_fill(act, ("lg", b - 1))
                did_read(act.activation(xn2_t, src.rearrange("p (c n) -> p c n", c=DCH), ACT.Identity), ("x2T", b))

            def context_copy(b, j):
                src = may_read(act, ("ct", b, j, 1))
                after_fill(act, ("s", b, j - 2) if j >= 2 else ("s", b - 1, j + 2))
                did_read(act.activation(ctx_t[:, j % 2, 1, :], src, ACT.Identity), ("ct", b, j, 1))

            context_copy(1, 0)
            softmax_exp(0)
            for b in range(NB):
                for j in range(NQ):
                    if j % 2 == 0:
                        src = may_read(act, ("pT", b, j))
                        if b > 0:
                            after_fill(act, ("pv", b - 1))
                        did_read(act.activation(probs_t[:, KPQ * j:KPQ * j + KPQ, :],
                                                src.rearrange("p (k n) -> p k n", k=KPQ), ACT.Identity),
                                 ("pT", b, j))
                    if b + 1 < NB and j + 1 < NQ:
                        context_copy(b + 1, j + 1)
                if b + 2 < NB:
                    context_copy(b + 2, 0)
                if b + 1 < NB:
                    softmax_exp(b + 1)
                if b == 2:
                    turned_gate_rows(0)
            def rows_high(b):
                act.wait_ge(xn2_ready, b + 1)
                act.activation(xn2_hi[b], xn2[:, b, :], ACT.Identity).then_inc(xn2_hi_ready, 1)

            turned_gate_rows(1)
            after_fill(act, ("pv", 3))
            rows_high(0)
            rows_high(1)
            turned_gate_rows(2)
            rows_high(2)
            turned_gate_rows(3)
            rows_high(3)
            after_fill(act, ("k3", 1))
            act.dma_start(b1_sb, b1).then_inc(bias_loaded, 16)
            act.wait_ge(lsub_ready, 1)
            act.activation(lexp, lsub, ACT.Exp).then_inc(lexp_ready, 1)
            act.wait_ge(windows_ready, 2)
            bounds = [act.value_load(win_i[0:1, e:e + 1], min_val=0, max_val=MAXW) for e in range(NE + 1)]
            for c in range(0, DCH, 2):
                sorted_tokens(act, c, lambda dst, src: act.activation(dst, src, ACT.Identity))

            def split_high(e, w, n):
                unit = unit_of(e, n)
                act.wait_ge(place_loaded[weight_place(unit)], 16 * weight_count(unit))
                act.wait_ge(parts_used, PARTS * (w + 1) + n - NSPLIT + 1)
                if n == 2:
                    after_fill(act, ("xs", DCH - 1))
                act.activation(w_hi[:, n % NSPLIT, :, :], weight_part(e, n), ACT.Identity).then_inc(hi_ready, 1)

            def outputs_copy(w):
                act.wait_ge(parts_used, PARTS * w + PARTS)
                act.wait_ge(rows_sent, 16 * w + 16)
                act.activation(y_out, bank[:, Y_BANK, :], ACT.Identity).then_inc(y_copied, 1)

            def block_copy(w, k):
                block_may_copy(act, 0, w, k)
                act.activation(hid[0], bank[:, H_BANK[0], :], ACT.Identity).then_inc(h_copied[0], 1)

            def block_relu(e, w, k):
                block_may_relu(act, 0, w, k)
                for i in range(HB_CH):
                    m = 2 * HB_CH * k + i
                    ins = act.activation(hid[0][:, i * P:(i + 1) * P], bank[:, T_BANK[0], i * P:(i + 1) * P], ACT.Relu,
                                         bias=b1_sb[:, e, m:m + 1])
                ins.then_inc(h_relu[0], 1)

            def block_high(w, i):
                p, k = i % 2, i // 2
                act.wait_ge(h_relu[p], 2 * w + k + 2)
                wait_block(act, w, "o", i - 2)
                act.activation(h_hi[:, p, :, :], hid[p].rearrange("p (m s) -> p m s", m=HB_CH), ACT.Identity) \
                    .then_inc(h_hi_ready[p], 1)

            act.wait_ge(bias_loaded, 16)
            act.wait_ge(rows_sent, 32)
            for e in range(NE):
                with act.If(bounds[e] < bounds[e + 1]):
                    with act.Fori(bounds[e], bounds[e + 1]) as w:
                        for n in range(4):
                            split_high(e, w, n)
                        outputs_copy(w)
                        for n in range(4, 6):
                            split_high(e, w, n)
                        block_copy(w, 0)
                        for n in range(6, 8):
                            split_high(e, w, n)
                        block_relu(e, w, 0)
                        block_high(w, 0)
                        for n in range(8, 10):
                            split_high(e, w, n)
                        block_high(w, 1)
                        for n in range(10, 12):
                            split_high(e, w, n)
                        block_copy(w, 1)
                        for n in range(12, 14):
                            split_high(e, w, n)
                        block_relu(e, w, 1)
                        block_high(w, 2)
                        for n in range(14, 16):
                            split_high(e, w, n)
                        block_high(w, 3)
            outputs_copy(bounds[NE])

        @block.vector
        def _(dve):
            steps = [0]

            def link(ins):
                steps[0] += 1
                ins.then_inc(dve_step, 1)
                dve.wait_ge(dve_step, steps[0])

            dve.memset(m_half, -0.5).then_inc(half_ready, 1)
            dve.wait_ge(dt_ready, 2)
            dve.tensor_scalar(step_mag, step_l, decay, -1.0, ALU.mult, ALU.mult).then_inc(step_mag_ready, 1)
            dve.tensor_scalar(step_ph, step_l, lam_c[:, 1:2], 1.0 / TWO_PI, ALU.mult, ALU.mult) \
                .then_inc(step_ph_ready, 1)

            def phases(turns, n, ready):
                dve.wait_ge(turns_ready, n)
                if n > 1:
                    dve.wait_ge(*((a_phase_ready, n - 1) if n <= AH // 2 + 1 else (b_phase_end_ready, n - AH // 2 - 1)))
                link(dve.tensor_scalar(round_v, turns, ROUND, None, ALU.add))
                dve.scalar_tensor_tensor(out=turns, in0=round_v, scalar=ROUND, in1=turns, op0=ALU.subtract,
                                         op1=ALU.subtract).then_inc(ready, 1)

            def a_phases(i):
                phases(a_sin[:, 2 * i:2 * i + 2, :], i + 1, a_phase_ready)

            norms = [0]

            def layer_norm(tiles, dst, meanwhile=None):
                n = len(tiles)
                for i, t in enumerate(tiles):
                    link(dve.bn_stats(bn6, x_sb[:, t, :]))
                    link(dve.bn_aggr(mv[:, 2 * i:2 * i + 2], bn6))
                var = mv.rearrange("p (t k) -> p t k", k=2)[:, 0:n, 1:2]
                dve.tensor_scalar(var_eps[:, 0:n].unsqueeze(2), var, EPS, None, ALU.add).then_inc(var_ready, 1)
                norms[0] += 1
                if meanwhile:
                    meanwhile()
                dve.wait_ge(rstd_ready, norms[0])
                for i, t in enumerate(tiles):
                    ins = dve.tensor_scalar(dst[i], x_sb[:, t, :], mv[:, 2 * i:2 * i + 1], rstd[:, i:i + 1],
                                            ALU.subtract, ALU.mult)
                return ins

            a_phases(0)
            dve.wait_ge(x_loaded, 16)
            layer_norm(range(NB), [xn1[:, b, :] for b in range(NB)], lambda: a_phases(1)).then_inc(xn1_ready, 1)
            dve.wait_ge(qk_loaded, 48)
            link(dve.tensor_tensor(bkq_prod, bkq_sb[:, :, 0], bkq_sb[:, :, 1], ALU.mult))
            dve.tensor_reduce(bkq_sum, bkq_prod, AX, ALU.add).then_inc(bkq_ready, 1)
            for d in range(DCH):
                src = may_read(dve, ("wqk", d))
                dve.tensor_copy(wqk[:, d, :], src[:, 0:DC])
                did_read(dve.tensor_copy(wqb[:, d:d + 1], src[:, DC:DC + 1]), ("wqk", d))
            src = may_read(dve, ("bias",))
            did_read(dve.tensor_copy(qbias, src[:, 0:3]), ("bias",))
            for b in range(NB):
                src = may_read(dve, ("xnT", b))
                did_read(dve.tensor_copy(xn1_t[:, :, b * P:(b + 1) * P], src.rearrange("p (c n) -> p c n", c=DCH)),
                         ("xnT", b))
            for i in range(2, AH // 2):
                a_phases(i)
            for r in range(B_POOL, BL, 2):
                phases(b_sin2[:, r:r + 2, :], (AH + r - B_POOL) // 2 + 1, b_phase_end_ready)

            def value_bias():
                dve.wait_ge(xn1_ready, 1)
                dve.wait_ge(bv_loaded, 16)
                link(dve.tensor_tensor(x_sb[:], x_sb[:], bv_sb.unsqueeze(1).to_broadcast([P, NB, D]), ALU.add))

            src = may_read(dve, ("qb",))
            after_read(dve, ("bias",))
            did_read(dve.tensor_scalar(q_bk, src[:, 0:NB], qbias[:, 2:3], None, ALU.add), ("qb",))

            def context_read(b, j):
                for c in range(CCH if b == 0 else 1):
                    src = may_read(dve, ("ct", b, j, c))
                    if j >= 2:
                        after_fill(dve, ("s", b, j - 2))
                    elif b > 0:
                        after_fill(dve, ("s", b - 1, j + 2))
                    did_read(dve.tensor_copy(ctx_t[:, j % 2, c, :], src), ("ct", b, j, c))

            def quarter_max(b, j):
                src = may_read(dve, ("s", b, j))
                return dve.tensor_reduce(qmax[:, NQ * b + j:NQ * b + j + 1], src, AX, ALU.max)

            def row_bias(b):
                link(dve.tensor_reduce(rmax, qmax[:, NQ * b:NQ * b + NQ], AX, ALU.max))
                link(dve.tensor_tensor(rmax_q, rmax, q_bk[:, b:b + 1], ALU.add))
                dve.tensor_tensor(nbias[:, b:b + 1], q_bk[:, b:b + 1], rmax_q, ALU.subtract).then_inc(rmax_ready, 1)

            def a_table(i):
                dve.wait_ge(mags_ready, 1)
                dve.wait_ge(a_sin_ready, i // 2 + 1)
                rows = slice(2 * i, 2 * i + 2)
                return dve.tensor_tensor(a_tab[:, rows, :], a_tab[:, rows, :], a_sin[:, rows, :], ALU.mult)

            context_read(0, 0)
            for j in range(NQ):
                if j + 1 < NQ:
                    context_read(0, j + 1)
                    a_table(j)
                ins = quarter_max(0, j)
            link(ins)
            row_bias(0)
            context_read(1, 0)
            for i in range(NQ - 1, AH // 2):
                ins = a_table(i)
            ins.then_inc(a_tab_ready, 1)

            def b_sum():
                dve.wait_ge(wi_done, 1)
                dve.wait_ge(wr_done, 1)
                dve.tensor_tensor(b_sin1, b_sin1, b_sin2, ALU.add).then_inc(b_sum_ready, 1)

            def b_table():
                dve.wait_ge(b_sum_ready, 1)
                dve.wait_ge(mags_ready, 1)
                dve.tensor_tensor(b_tab, b_tab, b_sin1, ALU.mult).then_inc(b_tab_ready, 1)

            def kernel_reads():
                own = table("own").unsqueeze(1).unsqueeze(1).to_broadcast([P, 8, BL, HG])
                for g in range(8):
                    src = may_read(dve, ("k1", g)).rearrange("p (g b h) -> p g b h", g=8, b=BL)
                    if g == 0:
                        dve.wait_ge(b_tab_ready, 1)
                    dst = k_parts.rearrange("p b (h g) -> p g b h", h=HG)[:, 8 * g:8 * g + 8, :, :]
                    did_read(dve.tensor_tensor(dst, src, own, ALU.mult), ("k1", g))
                src = may_read(dve, ("k2",))
                dve.wait_ge(b_phase_ready, (BL + B_POOL) // 2)
                link(dve.tensor_copy(k_time, src))
                dve.wait_ge(d_loaded, 16)
                did_read(dve.tensor_tensor(k_time[0:1, :], k_time[0:1, :], d_sb, ALU.add), ("k2",))
                for i in range(2):
                    src = may_read(dve, ("k3", i))
                    did_read(dve.tensor_copy(kfreq[:, i, :], src), ("k3", i))

            def attention_out(b):
                src = may_read(dve, ("pv", b))
                link(dve.tensor_reduce(rtot, rsum[:, NQ * b:NQ * b + NQ], AX, ALU.add))
                link(dve.reciprocal(rtot, rtot))
                if b == 0:
                    dve.wait_ge(b_phase_ready, (BL + B_POOL) // 2)
                did_read(dve.tensor_scalar(an, src[:, 0:DC], rtot, None, ALU.mult), ("pv", b))

            def values_turned(b):
                src = may_read(dve, ("anT", b))
                did_read(dve.tensor_copy(an_t, src[:, 0:DC].rearrange("p (c n) -> p c n", c=CCH)), ("anT", b))

            def values_added(b):
                src = may_read(dve, ("av", b))
                did_read(dve.tensor_tensor(x_sb[:, b, :], src, x_sb[:, b, :], ALU.add), ("av", b))
                after_read(dve, ("av", b))
                if b == 0:
                    dve.wait_ge(wr_done, 1)
                layer_norm([b], [u_sb]).then_inc(u_ready, 1)

            def freq_reads(b):
                uc, us = may_read(dve, ("uc", b)), may_read(dve, ("us", b))
                kc, ks = kfreq[:, 0, :], kfreq[:, 1, :]
                dve.tensor_tensor(prod1, uc, ks, ALU.mult)
                did_read(dve.tensor_tensor(y_cos, uc, kc, ALU.mult), ("uc", b))
                dve.tensor_tensor(prod2, us, ks, ALU.mult)
                did_read(dve.tensor_tensor(y_sin, us, kc, ALU.mult), ("us", b))
                after_read(dve, ("us", b))
                dve.tensor_tensor(y_cos, y_cos, prod2, ALU.subtract)
                dve.tensor_tensor(y_sin, y_sin, prod1, ALU.add).then_inc(spec_ready, 1)

            def time_reads(b):
                src = may_read(dve, ("y", b))
                did_read(dve.tensor_tensor(x_sb[:, b, :], src, x_sb[:, b, :], ALU.add), ("y", b))
                after_read(dve, ("y", b))
                layer_norm([b], [xn2[:, b, :]]).then_inc(xn2_ready, 1)

            def gate_reads(b):
                dve.wait_ge(gate_loaded, 32)
                src = may_read(dve, ("lg", b))
                did_read(dve.tensor_tensor(logits[:, b, :], src[:, 0:NE], bg_sb[:], ALU.add), ("lg", b))

            for b in range(NB):
                for j in range(NQ):
                    if j % 2:
                        src = may_read(dve, ("pT", b, j))
                        if b > 0:
                            after_fill(dve, ("pv", b - 1))
                        did_read(dve.tensor_copy(probs_t[:, KPQ * j:KPQ * j + KPQ, :],
                                                 src.rearrange("p (k n) -> p k n", k=KPQ)), ("pT", b, j))
                    if b + 1 < NB:
                        if j + 1 < NQ:
                            context_read(b + 1, j + 1)
                        ins = quarter_max(b + 1, j)
                if b + 1 < NB:
                    link(ins)
                    row_bias(b + 1)
                if b + 2 < NB:
                    context_read(b + 2, 0)
                if b == 0:
                    value_bias()
                    b_sum()
                if b >= 1:
                    values_turned(b - 1)
                    values_added(b - 1)
                if b == 1:
                    b_table()
                if b >= 2:
                    time_reads(b - 2)
                attention_out(b)
                if b == 1:
                    kernel_reads()
                if b == 3:
                    values_turned(3)
                if b >= 1:
                    freq_reads(b - 1)
                if b == 2:
                    gate_reads(0)
            def rows_low(b):
                dve.wait_ge(xn2_hi_ready, b + 1)
                dve.wait_ge(xn2_ready, b + 1)
                dve.tensor_tensor(xn2_lo[b], xn2[:, b, :], xn2_hi[b], ALU.subtract).then_inc(xn2_lo_ready, 1)

            values_added(3)
            gate_reads(1)
            time_reads(2)
            freq_reads(3)
            gate_reads(2)
            rows_low(0)
            rows_low(1)
            time_reads(3)
            rows_low(2)
            gate_reads(3)
            rows_low(3)

            def per_e(v):
                return v.unsqueeze(2).to_broadcast([P, NB, NE])

            after_read(dve, ("lg", 3))
            link(dve.tensor_reduce(lmax, logits, AX, ALU.max))
            link(dve.tensor_tensor(first, logits, per_e(lmax), ALU.is_equal))
            link(dve.tensor_tensor(first, first, table("rank_e").unsqueeze(1).to_broadcast([P, NB, NE]), ALU.mult))
            link(dve.tensor_reduce(fmax, first, AX, ALU.max))
            dve.tensor_tensor(hot, first, per_e(fmax), ALU.is_equal).then_inc(hot_ready, 1)
            dve.tensor_tensor(lsub, logits, per_e(lmax), ALU.subtract).then_inc(lsub_ready, 1)

            link(dve.memset(seq_before[:, 0, :], 0.0))
            src = may_read(dve, ("route",))
            ranks = src[:, 0:NB * NE].rearrange("p (b e) -> p b e", e=NE)
            seq_counts = src[:, NB * NE:2 * NB * NE].rearrange("p (b e) -> p b e", e=NE)
            for b in range(NB):
                link(dve.tensor_tensor(seq_before[:, b + 1, :], seq_before[:, b, :], seq_counts[:, b, :], ALU.add))
            counts = seq_before[:, NB, :]
            did_read(dve.tensor_tensor(slot_e, seq_before[:, 0:NB, :], ranks, ALU.add), ("route",))
            before = table("before_e").rearrange("p (e f) -> p e f", f=NE)
            link(dve.tensor_tensor(cum_prod, before, counts.unsqueeze(1).to_broadcast([P, NE + 1, NE]), ALU.mult))
            link(dve.tensor_reduce(off9, cum_prod, AX, ALU.add))
            dve.tensor_scalar(nwin, counts, P / 2 - 0.5, 1.0 / P, ALU.add, ALU.mult)
            after_read(dve, ("route",))
            link(dve.tensor_tensor(slot_e, slot_e, off9[:, 0:NE].unsqueeze(1).to_broadcast([P, NB, NE]), ALU.add))
            link(dve.tensor_tensor(slot_e, slot_e, hot, ALU.mult))
            link(dve.tensor_reduce(slot, slot_e, AX, ALU.add))
            link(dve.tensor_tensor(slot_k, slot.unsqueeze(2).to_broadcast([P, NB, NB]),
                                   table("blocks").unsqueeze(1).to_broadcast([P, NB, NB]), ALU.subtract))
            for b in range(NB):
                dve.tensor_tensor(onehot[:, b, :].rearrange("p (k s) -> p k s", k=NB),
                                  table("iota").unsqueeze(1).to_broadcast([P, NB, P]),
                                  slot_k[:, b, :].unsqueeze(2).to_broadcast([P, NB, P]), ALU.is_equal) \
                    .then_inc(onehot_ready, 1)
            link(dve.tensor_scalar(nwin, nwin, ROUND, None, ALU.add))
            link(dve.tensor_scalar(nwin, nwin, ROUND, None, ALU.subtract))
            link(dve.tensor_tensor(cum_prod, before, nwin.unsqueeze(1).to_broadcast([P, NE + 1, NE]), ALU.mult))
            link(dve.tensor_reduce(cum9, cum_prod, AX, ALU.add))
            dve.tensor_copy(win_i, cum9).then_inc(windows_ready, 1)
            dve.tensor_copy(off_i, off9[:, 0:NE]).then_inc(windows_ready, 1)
            dve.tensor_copy(row_i, slot).then_inc(rows_ready, 1)

            one_ahead = [*h_copied, *t_filled, *h_relu, *h_lo_ready, y_added]
            for i, s in enumerate(one_ahead + PARTS * [parts_used]):
                dve.memset(spare[:, i:i + 1], 0.0).then_inc(s, 1)

            dve.wait_ge(lexp_ready, 1)
            link(dve.tensor_reduce(psum_e, lexp, AX, ALU.add))
            link(dve.reciprocal(prob, psum_e))
            dve.memset(xs_t[:, :, NB * P:], 0.0).then_inc(pad_ready, 1)
            dve.wait_ge(windows_ready, 2)
            bounds = [dve.value_load(win_i[0:1, 0:1], min_val=0, max_val=MAXW)]
            bounds.append(dve.value_load(win_i[0:1, 1:2], min_val=0, max_val=MAXW))
            offset = dve.value_load(off_i[0:1, 0:1], min_val=0, max_val=NB * P)
            for c in range(1, DCH, 2):
                sorted_tokens(dve, c, dve.tensor_copy)

            for c in range(DCH):
                after_read(dve, ("xs", c))
            dve.wait_ge(pad_ready, 1)
            dve.wait_ge(bias_loaded, 16)

            def block_copy(w, k):
                block_may_copy(dve, 1, w, k)
                dve.tensor_copy(hid[1], bank[:, H_BANK[1], :]).then_inc(h_copied[1], 1)

            def block_relu(e, w, k):
                block_may_relu(dve, 1, w, k)
                for i in range(HB_CH):
                    m = HB_CH * (2 * k + 1) + i
                    ins = dve.tensor_scalar(hid[1][:, i * P:(i + 1) * P], bank[:, T_BANK[1], i * P:(i + 1) * P],
                                            b1_sb[:, e, m:m + 1], 0.0, ALU.add, ALU.max)
                ins.then_inc(h_relu[1], 1)

            def block_low(w, i):
                p, k = i % 2, i // 2
                dve.wait_ge(h_hi_ready[p], 2 * w + k + 1)
                dve.tensor_tensor(h_lo[:, p, :, :], hid[p].rearrange("p (m s) -> p m s", m=HB_CH), h_hi[:, p, :, :],
                                  ALU.subtract).then_inc(h_lo_ready[p], 1)

            def low_part(e, w, n):
                split_low(dve, e, w, n, lo_ready)

            for e in range(NE):
                if e > 0:
                    bounds.append(dve.value_load(win_i[0:1, e + 1:e + 2], min_val=0, max_val=MAXW))
                    offset = dve.value_load(off_i[0:1, e:e + 1], min_val=0, max_val=NB * P)
                with dve.If(bounds[e] < bounds[e + 1]):
                    with dve.Fori(bounds[e], bounds[e + 1]) as w:
                        x_win = xs_t[:, :, bass.ds(window_row(offset, w - bounds[e]), P)]
                        dve.tensor_copy(x_hi[:], x_win).then_inc(x_hi_ready, 1)
                        dve.wait_ge(x_hi_ready, w + 1)
                        dve.tensor_tensor(x_lo[:], x_win, x_hi[:], ALU.subtract).then_inc(xw_ready, 1)
                        for n in (0, 1, 2, 3, 4, 5, 7):
                            low_part(e, w, n)
                        block_copy(w, 0)
                        block_low(w, 0)
                        block_relu(e, w, 0)
                        for n in range(8, 10):
                            low_part(e, w, n)
                        block_low(w, 1)
                        for n in range(10, 12):
                            low_part(e, w, n)
                        block_copy(w, 1)
                        block_low(w, 2)
                        block_relu(e, w, 1)
                        low_part(e, w, 14)
                        block_low(w, 3)

            for b in range(NB):
                dve.wait_ge(gathered[b], 16)
                dve.scalar_tensor_tensor(out=x_sb[:, b, :], in0=y_tok[:, b, :], scalar=prob[:, b:b + 1],
                                         in1=x_sb[:, b, :], op0=ALU.mult, op1=ALU.add).then_inc(result_ready, 1)

        @block.gpsimd
        def _(pool):
            steps = [0]

            def link(ins):
                steps[0] += 1
                ins.then_inc(pool_step, 1)
                pool.wait_ge(pool_step, steps[0])

            def inverse_root(k):
                pool.wait_ge(var_ready, k)
                pool.tensor_tensor(rstd, var_eps, m_half, ALU.pow).then_inc(rstd_ready, 1)

            pool.wait_ge(dt_ready, 2)
            pool.wait_ge(step_ph_ready, 1)
            for i in range((BL + B_POOL) // 2):
                if i == 1:
                    pool.wait_ge(half_ready, 1)
                    inverse_root(1)
                dst, r = (b_sin1, b_sin2)[i // 4], 2 * (i % 4)
                turns = dst[:, r:r + 2, :]
                for k in (r, r + 1):
                    ins = pool.tensor_scalar(dst[:, k, :], dt_sb, step_ph[:, AH + k:AH + k + 1],
                                             phase_c[:, 1 + i // 4:2 + i // 4], ALU.mult, ALU.add)
                link(ins)
                link(pool.tensor_scalar(round_g, turns, ROUND, 1.0, ALU.add, ALU.mult))
                link(pool.tensor_scalar(round_g, round_g, -ROUND, 1.0, ALU.add, ALU.mult))
                pool.tensor_tensor(turns, round_g, turns, ALU.subtract).then_inc(b_phase_ready, 1)
            pool.wait_ge(b_phase_ready, (BL + B_POOL) // 2)
            pool.memset(y_out, 0.0).then_inc(zeros_ready, 1)
            pool.wait_ge(zeros_ready, 1)
            for i in range(2):
                rows = slice(i * P // 2, (i + 1) * P // 2)
                pool.dma_start(y_rows[NB * P:, :][rows], y_out[rows]).then_inc(rows_sent, 16)
            pool.wait_ge(b_sin_ready, 2)
            pool.wait_ge(wri_loaded, 16)
            pool.tensor_tensor(b_sin1, b_sin1, wri[:, 0, :].unsqueeze(1).to_broadcast([P, BL, D]), ALU.mult) \
                .then_inc(wr_done, 1)
            pool.wait_ge(b_sin_ready, 4)
            pool.tensor_tensor(b_sin2, b_sin2, wri[:, 1, :].unsqueeze(1).to_broadcast([P, BL, D]), ALU.mult) \
                .then_inc(wi_done, 1)
            for k in range(2 * NB):
                inverse_root(k + 2)

            pool.wait_ge(windows_ready, 2)
            bounds = [pool.value_load(win_i[0:1, e:e + 1], min_val=0, max_val=MAXW) for e in range(NE + 1)]
            offsets = [pool.value_load(off_i[0:1, e:e + 1], min_val=0, max_val=NB * P) for e in range(NE)]
            for e in range(NE):
                pool.wait_ge(b2_loaded[e % NB2], 16 * (e // NB2 + 1))
                with pool.If(bounds[e] < bounds[e + 1]):
                    with pool.Fori(bounds[e], bounds[e + 1]) as w:
                        first_row = window_row(offsets[e], w - bounds[e])
                        for n in LOW_BY_GPSIMD:
                            split_low(pool, e, w, n, lo_ready_pool)
                        pool.wait_ge(y_copied, w + 2)
                        pool.tensor_tensor(y_out, y_out, b2_sb[e % NB2], ALU.add).then_inc(y_added, 1)
                        pool.wait_ge(y_added, w + 2)
                        pool.dma_start(y_rows[bass.ds(first_row, P), :], y_out).then_inc(rows_sent, 16)
            pool.wait_ge(rows_sent, 16 * bounds[NE] + 32)
            pool.tensor_tensor(rstd, m_half, m_half, ALU.mult)
            pool.wait_ge(rows_ready, 1)
            for b in range(NB):
                pool.indirect_dma_start(y_tok[:, b, :], None, y_rows,
                                        bass.IndirectOffsetOnAxis(ap=row_i[:, b:b + 1], axis=0)) \
                    .then_inc(gathered[b], 16)

        @block.tensor
        def _(pe):
            def col_slice(c):
                return slice(c * P, (c + 1) * P)

            pe.wait_ge(qk_loaded, 48)
            for d in range(DCH):
                dst = may_fill(pe, ("wqk", d))
                for e in range(DCH):
                    pe.matmul(dst[:, 0:DC], wq_sb[:, e, col_slice(d)], wk_sb[:, e, :], start=e == 0, stop=e == DCH - 1)
                for e in range(DCH):
                    ins = pe.matmul(dst[:, DC:DC + 1], wq_sb[:, e, col_slice(d)], bkq_sb[:, e, 0:1],
                                    start=e == 0, stop=e == DCH - 1)
                did_fill(ins, ("wqk", d))
            dst = may_fill(pe, ("bias",))
            for c in range(CCH):
                for e in range(DCH):
                    pe.matmul(dst[:, c:c + 1], wk_sb[:, e, col_slice(c)], bkq_sb[:, e, 1:2],
                              start=e == 0, stop=e == DCH - 1)
            pe.wait_ge(tab_loaded, 16)
            pe.wait_ge(bkq_ready, 1)
            did_fill(pe.matmul(dst[:, 2:3], ones, bkq_sum, start=True, stop=True), ("bias",))
            pe.wait_ge(xn1_ready, 1)
            for b in range(NB):
                dst = may_fill(pe, ("xnT", b))
                for c in range(DCH):
                    ins = pe.transpose(dst[:, col_slice(c)], xn1[:, b, col_slice(c)], ident)
                did_fill(ins, ("xnT", b))
            for d in range(DCH):
                after_read(pe, ("wqk", d))
            for b in range(NB):
                after_read(pe, ("xnT", b))
            for c in range(CCH):
                dst = may_fill(pe, ("q", c))
                for d in range(DCH):
                    ins = pe.matmul(dst, wqk[:, d, col_slice(c)], xn1_t[:, d, :], start=d == 0, stop=d == DCH - 1)
                did_fill(ins, ("q", c))
            dst = may_fill(pe, ("qb",))
            for b in range(NB):
                for d in range(DCH):
                    ins = pe.matmul(dst[:, b:b + 1], xn1_t[:, d, col_slice(b)], wqb[:, d:d + 1],
                                    start=d == 0, stop=d == DCH - 1)
            did_fill(ins, ("qb",))

            def turn_context(b, j):
                if j == 0:
                    pe.wait_ge(place_loaded[b], 16)
                for c in range(CCH):
                    dst = may_fill(pe, ("ct", b, j, c))
                    for k in range(KPQ):
                        ins = pe.transpose(dst[:, col_slice(k)], ctx_sb[b][:, KPQ * j + k, col_slice(c)], ident)
                    did_fill(ins, ("ct", b, j, c))

            def scores(b, j):
                dst = may_fill(pe, ("s", b, j))
                for c in range(CCH):
                    if b == 0 and j == 0:
                        after_read(pe, ("q", c))
                    after_read(pe, ("ct", b, j, c))
                    ins = pe.matmul(dst, q_t[:, c, col_slice(b)], ctx_t[:, j % 2, c, :],
                                    start=c == 0, stop=c == CCH - 1)
                did_fill(ins, ("s", b, j))

            def turn_probs(b, j):
                after_read(pe, ("s", b, j))
                dst = may_fill(pe, ("pT", b, j))
                for k in range(KPQ):
                    ins = pe.transpose(dst[:, col_slice(k)], probs[:, col_slice(KPQ * j + k)], ident)
                did_fill(ins, ("pT", b, j))

            def probs_context(b):
                dst = may_fill(pe, ("pv", b))
                for j in range(NQ):
                    after_read(pe, ("pT", b, j))
                    for k in range(KPQ * j, KPQ * j + KPQ):
                        ins = pe.matmul(dst[:, 0:DC], probs_t[:, k, :], ctx_sb[b][:, k, :],
                                        start=k == 0, stop=k == KCH - 1)
                did_fill(ins, ("pv", b))

            def kernel_products():
                pe.wait_ge(a_tab_ready, 1)
                pe.wait_ge(b_tab_ready, 1)
                a_cols = a_tab.rearrange("p a (h g) -> p (a h) g", h=HG)
                b_cols = b_tab.rearrange("p b (h g) -> p (b h) g", h=HG)
                for g in range(8):
                    dst = may_fill(pe, ("k1", g))
                    for i in range(8):
                        ins = pe.matmul(dst[:, i * BL * HG:(i + 1) * BL * HG], a_cols[:, :, 8 * g + i],
                                        b_cols[:, :, 8 * g + i], start=True, stop=True)
                    did_fill(ins, ("k1", g))
                dst = may_fill(pe, ("k2",))
                after_read(pe, ("k1", 6))
                after_read(pe, ("k1", 7))
                pick = table("pick")
                for i in range(BL):
                    ins = pe.matmul(dst, pick[:, BL - 1 - i:BL - 1 - i + P], k_parts[:, i, :],
                                    start=i == 0, stop=i == BL - 1)
                did_fill(ins, ("k2",))
                after_read(pe, ("k2",))
                for i in range(2):
                    dst = may_fill(pe, ("k3", i))
                    did_fill(pe.matmul(dst, table(("cos_f", "sin_f")[i]), k_time, start=True, stop=True), ("k3", i))

            def values(b):
                dst = may_fill(pe, ("anT", b))
                after_read(pe, ("pv", b))
                for c in range(CCH):
                    ins = pe.transpose(dst[:, col_slice(c)], an[:, col_slice(c)], ident)
                did_fill(ins, ("anT", b))
                dst = may_fill(pe, ("av", b))
                pe.wait_ge(wv_loaded, 16)
                after_read(pe, ("anT", b))
                for c in range(CCH):
                    ins = pe.matmul(dst, an_t[:, c, :], wv_sb[:, c, :], start=c == 0, stop=c == CCH - 1)
                did_fill(ins, ("av", b))

            def to_frequency(b):
                pe.wait_ge(u_ready, b + 1)
                for what, name in ((("uc", b), "cos_f"), (("us", b), "sin_f")):
                    dst = may_fill(pe, what)
                    did_fill(pe.matmul(dst, table(name), u_sb, start=True, stop=True), what)

            def to_time(b):
                pe.wait_ge(spec_ready, b + 1)
                dst = may_fill(pe, ("y", b))
                pe.matmul(dst, table("cos_t"), y_cos, start=True, stop=False)
                did_fill(pe.matmul(dst, table("sin_t"), y_sin, start=False, stop=True), ("y", b))

            def gate(b):
                pe.wait_ge(xn2_ready, b + 1)
                dst = may_fill(pe, ("x2T", b))
                for c in range(DCH):
                    ins = pe.transpose(dst[:, col_slice(c)], xn2[:, b, col_slice(c)], ident)
                did_fill(ins, ("x2T", b))
                dst = may_fill(pe, ("lg", b))
                pe.wait_ge(gate_loaded, 32)
                after_read(pe, ("x2T", b))
                for c in range(DCH):
                    ins = pe.matmul(dst[:, 0:NE], xn2_t[:, c, :], wg_sb[:, c, :], start=c == 0, stop=c == DCH - 1)
                did_fill(ins, ("lg", b))

            turn_context(0, 0)
            for j in range(NQ):
                if j + 1 < NQ:
                    turn_context(0, j + 1)
                scores(0, j)
            turn_context(1, 0)
            for b in range(NB):
                for j in range(NQ):
                    turn_probs(b, j)
                    if b + 1 < NB:
                        if j + 1 < NQ:
                            turn_context(b + 1, j + 1)
                        scores(b + 1, j)
                if b + 2 < NB:
                    turn_context(b + 2, 0)
                if b >= 1:
                    values(b - 1)
                if b >= 2:
                    to_time(b - 2)
                probs_context(b)
                if b == 1:
                    kernel_products()
                if b >= 1:
                    to_frequency(b - 1)
                if b == 2:
                    gate(0)
            values(3)
            gate(1)
            to_time(2)
            to_frequency(3)
            gate(2)
            to_time(3)
            gate(3)

            dst = may_fill(pe, ("route",))
            pe.wait_ge(hot_ready, 1)
            pe.matmul(dst[:, 0:NB * NE], table("earlier"), hot_2d, start=True, stop=True)
            ins = pe.matmul(dst[:, NB * NE:2 * NB * NE], ones, hot_2d, start=True, stop=True)
            did_fill(ins, ("route",))

            for c in range(DCH):
                dst = may_fill(pe, ("xs", c))
                for b in range(NB):
                    pe.wait_ge(onehot_ready, b + 1)
                    pe.wait_ge(xn2_lo_ready, b + 1)
                    pe.matmul(dst, xn2_hi[b][:, col_slice(c)], onehot[:, b, :], start=b == 0, stop=False)
                    ins = pe.matmul(dst, xn2_lo[b][:, col_slice(c)], onehot[:, b, :], start=False, stop=b == NB - 1)
                did_fill(ins, ("xs", c))

            def products(e, w, what, i, dst, rows, start, stop):
                for g in range(2):
                    n = 2 * BLOCKS.index((what, i)) + g
                    in_pool = [m for m in LOW_BY_GPSIMD if m <= n]
                    if n in LOW_BY_GPSIMD:
                        pe.wait_ge(lo_ready_pool, len(LOW_BY_GPSIMD) * w + len(in_pool))
                    else:
                        pe.wait_ge(lo_ready, (PARTS - len(LOW_BY_GPSIMD)) * w + n + 1 - len(in_pool))
                    terms = [(x, part, c) for x, part in ((0, w_hi), (1, w_hi), (0, w_lo)) for c in range(2)]
                    for q, (x, part, c) in enumerate(terms):
                        ins = pe.matmul(dst, rows(x, 2 * g + c), part[:, n % NSPLIT, c, :],
                                        start=start and g == 0 and q == 0, stop=stop and g == 1 and q == len(terms) - 1)
                    ins.then_inc(parts_used, 1)

            def hidden(e, w, i):
                p, k = i % 2, i // 2
                pe.wait_ge(h_copied[p], 2 * w + k + 1)
                products(e, w, "h", i, bank[:, H_BANK[p], :], lambda x, d: (x_hi, x_lo)[x][:, d, :], True, True)

            def turn_hidden(w, i):
                p, k = i % 2, i // 2
                pe.wait_ge(h_copied[p], 2 * w + k + 2)
                pe.wait_ge(h_relu[p], 2 * w + k + 1)
                for c in range(HB_CH):
                    ins = pe.transpose(bank[:, T_BANK[p], col_slice(c)], hid[p][:, col_slice(c)], ident)
                ins.then_inc(t_filled[p], 1)

            def output(e, w, i):
                p, k = i % 2, i // 2
                pe.wait_ge(h_lo_ready[p], 2 * w + k + 2)
                products(e, w, "o", i, bank[:, Y_BANK, :], lambda x, c: (h_hi, h_lo)[x][:, p, c, :], i == 0, i == 3)

            pe.wait_ge(windows_ready, 2)
            bounds = [pe.value_load(win_i[0:1, e:e + 1], min_val=0, max_val=MAXW) for e in range(NE + 1)]
            for b in range(8):
                pe.wait_ge(drained[b], FILL_COUNT[b])
            for e in range(NE):
                with pe.If(bounds[e] < bounds[e + 1]):
                    with pe.Fori(bounds[e], bounds[e + 1]) as w:
                        pe.wait_ge(xw_ready, w + 1)
                        hidden(e, w, 0)
                        hidden(e, w, 1)
                        turn_hidden(w, 0)
                        hidden(e, w, 2)
                        turn_hidden(w, 1)
                        pe.wait_ge(y_copied, w + 1)
                        output(e, w, 0)
                        hidden(e, w, 3)
                        turn_hidden(w, 2)
                        output(e, w, 1)
                        turn_hidden(w, 3)
                        output(e, w, 2)
                        output(e, w, 3)


def shape_tables():
    import numpy as np

    t = np.zeros((P, TABLE_COLS), np.float32)

    def put(name, value):
        lo, hi = TABLES[name]
        t[:, lo:hi] = value

    p = np.arange(P)
    angle = np.pi * (((2 * p[None, :] + 1) * p[:, None]) % (4 * P)) / (2 * P)
    put("ident", np.eye(P))
    put("ones", 1.0)
    put("cos_f", np.cos(angle))
    put("sin_f", np.sin(angle))
    put("cos_t", np.cos(angle.T) / P)
    put("sin_t", np.sin(angle.T) / P)
    put("pick", np.arange(P + BL - 1)[None, :] == (BL * (p // HG) + BL - 1)[:, None])
    put("own", np.arange(HG)[None, :] == (p % HG)[:, None])
    put("earlier", p[:, None] < p[None, :])
    put("iota", np.arange(P))
    put("blocks", P * np.arange(NB))
    put("rank_e", NE - np.arange(NE))
    put("before_e", (np.arange(NE)[None, :] < np.arange(NE + 1)[:, None]).ravel())
    return t


def time_tables():
    import numpy as np

    p = np.arange(P)
    times = np.tile(np.concatenate([BL * np.arange(AH), np.arange(BL)]), (P, 1))
    turns = np.where(p[:, None] < NS, [[0.25, 0.25, 0.5]], [[0.0, 0.5, 0.75]])
    return np.concatenate([times, turns], 1).astype(np.float32)


def kernel(**inputs):
    import numpy as np
    import concourse.bacc as bacc
    from concourse.bass_utils import run_bass_kernel_spmd

    g = {k: np.asarray(v) for k, v in inputs.items()}
    nc = bacc.Bacc("TRN2", target_bir_lowering=False, num_devices=1)
    w_re_t, w_im_t = g["L0_attn_W_re"].T, g["L0_attn_W_im"].T
    lam = np.stack([g["L0_attn_Lambda_re"], g["L0_attn_Lambda_im"]], 1)
    arrays = {
        "x": g["x"].reshape(NB * LQ, D),
        "ctx": g["ctx_512"],
        "wq_t": g["L0_xattn_Wq"].T,
        "wk_t": g["L0_xattn_Wk"].T,
        "bkq": np.stack([g["L0_xattn_bk"], g["L0_xattn_bq"]], 1),
        "wv": g["L0_xattn_Wv"],
        "bv": g["L0_xattn_bv"],
        "log_dt": g["L0_attn_log_dt"],
        "w_ri": np.stack([np.concatenate([w_re_t, w_re_t]), np.concatenate([w_im_t, w_im_t])]),
        "lam": np.concatenate([lam, lam]),
        "d_skip": g["L0_attn_D"].reshape(1, D),
        "w_gate": g["L0_ffn_w_gate"],
        "b_gate": g["L0_ffn_b_gate"],
        "w1": g["L0_ffn_W1"],
        "b1": g["L0_ffn_b1"].reshape(NE, MCH, P).transpose(2, 0, 1),
        "w2": g["L0_ffn_W2"],
        "b2": g["L0_ffn_b2"],
        "times": time_tables(),
        "tables": shape_tables(),
    }
    arrays = {f"in_{k}": np.ascontiguousarray(v) for k, v in arrays.items()}
    args = [nc.dram_tensor(k, v.shape, mybir.dt.from_np(v.dtype), kind="ExternalInput").ap()
            for k, v in arrays.items()]
    out = nc.dram_tensor("out", (NB * LQ, D), F32, kind="ExternalOutput").ap()
    perceiver_layer(nc, *args, out)
    r = run_bass_kernel_spmd(nc, [arrays], core_ids=[0])
    return r.results[0]["out"].reshape(NB, LQ, D)
```
